# Optimizing a Trainium2 kernel written in Bass

```python
import numpy as np
import jax
import jax.numpy as jnp

def _softmax(x, axis=-1):
    return jax.nn.softmax(x, axis=axis)

def _gelu(x):
    return jax.nn.gelu(x, approximate=True)

def _silu(x):
    return jax.nn.silu(x)

def _sigmoid(x):
    return jax.nn.sigmoid(x)

def _layernorm(x, axis=-1, eps=1e-05):
    m = jnp.mean(x, axis=axis, keepdims=True)
    v = jnp.var(x, axis=axis, keepdims=True)
    return (x - m) / jnp.sqrt(v + eps)

def _scatter_add(tgt, idx, src, axis=0):
    return tgt.at[idx].add(src)

def _segment_sum(src, seg, n):
    return jax.ops.segment_sum(src, seg, n)
kernel_name = 'mk_conv_preact_d1_conv_nhwc16_r2_6c1e6b'

def setup_inputs(seed: int=0):
    np.random.seed(seed)
    _w = jnp.asarray

    def _rec_inputs():
        import jax
        import jax.numpy as jnp
        _gk = jax.random.key(seed)
        x = -0.0002928 + 1 * jax.random.normal(jax.random.fold_in(_gk, 1), (8, 256, 32, 16), jnp.float32)
        return x
    x = _rec_inputs()

    def _L0_conv_setup():
        import jax, jax.numpy as jnp
        import numpy as np
        B, S, C_IN, M = (8, 256, 32, 16)
        C_OUT, N_HEADS = (32, 8)
        C_H = C_OUT * N_HEADS

        def _mv_linear(x, W, b):
            return jnp.einsum('oc,bscm->bsom', W, x) + b[None, None, :, None]
        key = jax.random.key(seed)
        ks = jax.random.split(key, 9)
        scale = 0.02
        return {'x': jax.random.normal(ks[0], (B, S, C_IN, M), dtype=jnp.float32), 'Wq': jax.random.normal(ks[1], (C_H, C_IN), dtype=jnp.float32) * scale, 'bq': jnp.zeros((C_H,), dtype=jnp.float32), 'Wk': jax.random.normal(ks[2], (C_H, C_IN), dtype=jnp.float32) * scale, 'bk': jnp.zeros((C_H,), dtype=jnp.float32), 'Wv': jax.random.normal(ks[3], (C_H, C_IN), dtype=jnp.float32) * scale, 'bv': jnp.zeros((C_H,), dtype=jnp.float32), 'Wo': jax.random.normal(ks[4], (C_OUT, C_H), dtype=jnp.float32) * scale, 'bo': jnp.zeros((C_OUT,), dtype=jnp.float32)}
    _L0_conv_all = _L0_conv_setup()
    _L0_conv_in = {k: v for k, v in _L0_conv_all.items() if k in ('Wq', 'bq', 'Wk', 'bk', 'Wv', 'bv', 'Wo', 'bo')}
    del _L0_conv_all
    return {'x': x, 'L0_conv_Wq': _L0_conv_in['Wq'], 'L0_conv_bq': _L0_conv_in['bq'], 'L0_conv_Wk': _L0_conv_in['Wk'], 'L0_conv_bk': _L0_conv_in['bk'], 'L0_conv_Wv': _L0_conv_in['Wv'], 'L0_conv_bv': _L0_conv_in['bv'], 'L0_conv_Wo': _L0_conv_in['Wo'], 'L0_conv_bo': _L0_conv_in['bo']}

def reference(x, L0_conv_Wq, L0_conv_bq, L0_conv_Wk, L0_conv_bk, L0_conv_Wv, L0_conv_bv, L0_conv_Wo, L0_conv_bo):
    import jax
    import jax.numpy as jnp

    def _L0_conv_ref(x, Wq, bq, Wk, bk, Wv, bv, Wo, bo):
        import jax, jax.numpy as jnp
        import numpy as np
        B, S, C_IN, M = (8, 256, 32, 16)
        C_OUT, N_HEADS = (32, 8)
        C_H = C_OUT * N_HEADS

        def _mv_linear(x, W, b):
            return jnp.einsum('oc,bscm->bsom', W, x) + b[None, None, :, None]
        Q = _mv_linear(x, Wq, bq)
        K = _mv_linear(x, Wk, bk)
        V = _mv_linear(x, Wv, bv)
        Vp = jnp.transpose(V, (0, 3, 1, 2))
        Kt = jnp.transpose(K, (0, 3, 1, 2))
        Qp = jnp.transpose(Q, (0, 3, 2, 1))
        QK = Qp @ Kt
        A = jax.nn.softmax(QK, axis=-1)
        out = jnp.einsum('bmcC,bmsC->bsCm', A, Vp)
        return _mv_linear(out, Wo, bo)

    def _gn(v, G=8, eps=1e-05):
        B_, H_, W_, C_ = v.shape
        g = v.reshape(B_, H_, W_, G, C_ // G)
        m = jnp.mean(g, axis=(1, 2, 4), keepdims=True)
        s = jnp.var(g, axis=(1, 2, 4), keepdims=True)
        return ((g - m) / jnp.sqrt(s + eps)).reshape(v.shape)

    def _ln_c(v, eps=1e-06):
        m = jnp.mean(v, axis=-1, keepdims=True)
        s = jnp.var(v, axis=-1, keepdims=True)
        return (v - m) / jnp.sqrt(s + eps)

    def _ln_t(v, eps=1e-05):
        m = jnp.mean(v, axis=-1, keepdims=True)
        s = jnp.var(v, axis=-1, keepdims=True)
        return (v - m) / jnp.sqrt(s + eps)

    def _to_tokens(v):
        B_, H_, W_, C_ = v.shape
        return v.reshape(B_, H_ * W_, C_)

    def _from_tokens(t, like):
        return t.reshape(like.shape)
    x = x + _L0_conv_ref(_gn(x), L0_conv_Wq, L0_conv_bq, L0_conv_Wk, L0_conv_bk, L0_conv_Wv, L0_conv_bv, L0_conv_Wo, L0_conv_bo)
    return x

_drawn_inputs = setup_inputs


def setup_inputs(seed=0):
    import zlib

    import numpy as np

    out = dict(_drawn_inputs(seed))
    spreads = {'L0_conv_bq': (0.0, 0.388),
     'L0_conv_bk': (0.0, 0.338),
     'L0_conv_bv': (0.0, 0.1),
     'L0_conv_bo': (0.0, 0.1)}
    factors = {'L0_conv_Wq': 8.0, 'L0_conv_Wk': 3.111}
    for name, (base, spread) in spreads.items():
        noise = np.random.default_rng([zlib.crc32(name.encode()), seed]).standard_normal(out[name].shape)
        drawn = base * np.exp(spread * noise) if base else spread * noise
        out[name] = jnp.asarray(drawn.astype(out[name].dtype))
    for name, factor in factors.items():
        out[name] = (out[name] * factor).astype(out[name].dtype)
    return out
```

```python
import numpy as np
from contextlib import ExitStack

import concourse.bass as bass
from concourse import mybir

B, S, C, M = 8, 256, 32, 16
CH = 256
G = 8
P = 128
Q = P // C
T = M // Q
SC = S // P
HC = CH // P
PER_GROUP = S * C * (M // G)
EPS = 1e-5
LO = C
ST = 3 * C + 3

DIAG = 0
SAME = DIAG + C
MEAN = SAME + P
PICK = MEAN + 2 * P
ONES = PICK + M
LOMASK = ONES + C
OWN = LOMASK + 1
NCONST = OWN + Q


def shape_constants():
    p = np.arange(P)
    k = np.zeros((P, NCONST), np.float32)
    k[p, DIAG + p % C] = 1.0
    k[:, SAME:SAME + P] = (p[:, None] // (2 * C) == p[None, :] // (2 * C)) / PER_GROUP
    for hf in range(2):
        rows = (p // C) % 2 == hf
        k[rows, MEAN + hf * P:MEAN + (hf + 1) * P] = -1.0 / (PER_GROUP * C)
    for m in range(M):
        k[C * (m % Q) + m // Q, PICK + m] = 1.0
    k[:, ONES:ONES + C] = 1.0
    k[2 * C:3 * C, LOMASK] = -1.0
    k[3 * C + 2, LOMASK] = -1.0
    k[p, OWN + p // C] = 1.0
    return k


def build(nc, x_rows, x_cols, wq_stack, wk_rep, bk_rep, wv, wo, bv, bo_rep, consts, y_cols):
    f32 = mybir.dt.float32
    f32r = mybir.dt.float32r
    ALU = mybir.AluOpType
    ACT = mybir.ActivationFunctionType
    AX = mybir.AxisListType

    NS = 4
    AHEAD = 2
    RLAG = 2
    CLAG = 3
    NSTACK = 3 * Q + 3

    ctx = ExitStack()
    with ctx:
        def sb(name, shape, dt=f32):
            return ctx.enter_context(nc.sbuf_tensor(name, shape, dt))

        def bank(name):
            return ctx.enter_context(nc.psum_tensor(name, [P, 512], f32))

        def sem(name):
            return ctx.enter_context(nc.semaphore(name))

        k_sb = sb("k_sb", [P, NCONST])
        wq_raw = sb("wq_raw", [ST, CH])
        wq_hi = sb("wq_hi", [ST, CH], f32r)
        wq_st = sb("wq_st", [ST, CH], f32r)
        wk_sb = sb("wk_sb", [P, CH])
        bk_sb = sb("bk_sb", [P, CH])
        bk_all = sb("bk_all", [M, CH])
        wv_sb = sb("wv_sb", [P, HC, C])
        wo_sb = sb("wo_sb", [P, HC, C])
        wobv = sb("wobv", [P, HC, Q, C])
        bv_sb = sb("bv_sb", [P, HC])
        bo_sb = sb("bo_sb", [P, 1])
        half = sb("half", [P, T])
        xs = sb("xs", [P, SC, M, C])
        xT = sb("xT", [P, B, T, S])
        xc = sb("xc", [P, SC, M, C + 1])
        xcT = sb("xcT", [P, T, S])
        part = sb("part", [P, G // 2])
        nm = sb("nm", [P, G])
        nmT = sb("nmT", [P, B, T])
        gram = sb("gram", [P, T, C + 1])
        gdiag = sb("gdiag", [P, T, C])
        trace = sb("trace", [P, T])
        vare = sb("vare", [P, T])
        rs2 = sb("rs2", [P, T])
        rs = sb("rs", [P, B, T])
        rs_now = sb("rs_now", [P, T])
        gnorm = sb("gnorm", [P, T, C])
        ssum = sb("ssum", [P, T])
        gblk = sb("gblk", [P, T, Q, C])
        sblk = sb("sblk", [P, T, Q])
        t_sb = sb("t_sb", [P, T, CH])
        t_hi = sb("t_hi", [P, T, CH], f32r)
        t_lo = sb("t_lo", [P, T, CH], f32r)
        tb_sb = sb("tb_sb", [M, CH])
        tb_hi = sb("tb_hi", [M, CH], f32r)
        tb_lo = sb("tb_lo", [M, CH], f32r)
        stack = sb("stack", [ST, 2, M, CH], f32r)
        negmax = sb("negmax", [P, NS, HC])
        rowsum = sb("rowsum", [P, NS, HC])
        e_sb = sb("e_sb", [P, NS, HC, CH])
        recip = sb("recip", [P, T, Q, HC, C])
        a_sb = sb("a_sb", [P, CH])
        aT = sb("aT", [P, HC, M])
        ws = sb("ws", [P, HC, T, Q, C])
        wf = sb("wf", [P, T, C])
        wblk = sb("wblk", [P, T, Q, C])
        beff = sb("beff", [P, T])
        yb = sb("yb", [P, T, S])
        yo = sb("yo", [P, T, S])

        s_bank = [bank(f"s_bank{i}") for i in range(NS)]
        acc = bank("acc")
        bx = bank("bx")
        by = bank("by")
        bz = bank("bz")

        k_loaded = sem("k_loaded")
        w_loaded = sem("w_loaded")
        xs_loaded = sem("xs_loaded")
        xT_loaded = sem("xT_loaded")
        set_pool = sem("set_pool")
        set_dve = sem("set_dve")
        part_mm = sem("part_mm")
        part_done = sem("part_done")
        mean_mm = sem("mean_mm")
        mean_done = sem("mean_done")
        centred = sem("centred")
        gram_mm = sem("gram_mm")
        gram_done = sem("gram_done")
        diag_done = sem("diag_done")
        trace_done = sem("trace_done")
        var_mm = sem("var_mm")
        vare_done = sem("vare_done")
        var_done = sem("var_done")
        rs_done = sem("rs_done")
        pool_step = sem("pool_step")
        gblk_done = sem("gblk_done")
        t01_mm = sem("t01_mm")
        t23_mm = sem("t23_mm")
        tb_mm = sem("tb_mm")
        t01_done = sem("t01_done")
        t23_done = sem("t23_done")
        tb_done = sem("tb_done")
        hi_done = sem("hi_done")
        parts_done = sem("parts_done")
        stacked = sem("stacked")
        scores = sem("scores")
        maxed = sem("maxed")
        exped = sem("exped")
        inverted = sem("inverted")
        summed = sem("summed")
        acc_read = sem("acc_read")
        a_mm = sem("a_mm")
        a_done = sem("a_done")
        ws_done = sem("ws_done")
        xcT_done = sem("xcT_done")
        w_mm = sem("w_mm")
        wf_done = sem("wf_done")
        wblk_done = sem("wblk_done")
        y01_mm = sem("y01_mm")
        y23_mm = sem("y23_mm")
        yb_done = sem("yb_done")
        yo_done = sem("yo_done")
        y_stored = sem("y_stored")

        def after(eng, s, count):
            if not (isinstance(count, int) and count <= 0):
                eng.wait_ge(s, count)

        def settled(eng):
            eng.nop(nofuse=True)

        diag_m = k_sb[:, DIAG:DIAG + C]
        same_m = k_sb[:, SAME:SAME + P]
        pick_m = k_sb[:, PICK:PICK + M]
        own_m = k_sb[:, OWN:OWN + Q]
        ones_m = k_sb[:, ONES:ONES + C]

        block = ctx.enter_context(nc.Block())

        @block.sync
        def _(sp):
            def load_rows(j):
                after(sp, centred, j)
                settled(sp)
                after(sp, part_mm, j)
                settled(sp)
                sp.dma_start(xs[:, :, :, :], x_rows[bass.ds(j, 1)].rearrange("b (h p) m c -> p (b h) m c", p=P)
                             ).then_inc(xs_loaded, 16)

            def load_cols(j):
                after(sp, xcT_done, j)
                settled(sp)
                sp.dma_start(xT[:, bass.ds(j, 1), :, :], x_cols[bass.ds(j, 1)].rearrange("b t p s -> p b t s")
                             ).then_inc(xT_loaded, 16)

            def stack_up(j, side):
                after(sp, scores, M * (j - 1))
                settled(sp)
                sp.wait_ge(parts_done, j + 1)
                settled(sp)
                for row, part_of in ((0, t_hi), (C, t_lo), (2 * C, t_hi)):
                    for q in range(Q):
                        dst = stack[row:row + C, side, q:M:Q, :]
                        sp.dma_start(dst.bitcast(f32), part_of[C * q:C * q + C, :, :].bitcast(f32)).then_inc(stacked, 16)
                for row, part_of in ((3 * C, tb_hi), (3 * C + 1, tb_lo), (3 * C + 2, tb_hi)):
                    dst = stack[row:row + 1, side, :, :]
                    sp.dma_start(dst.bitcast(f32), part_of[:, :].bitcast(f32)).then_inc(stacked, 16)

            def store(j):
                sp.wait_ge(yo_done, j + 1)
                settled(sp)
                sp.dma_start(y_cols[bass.ds(j, 1)].rearrange("b t p s -> p b t s"), yo[:, None, :, :]
                             ).then_inc(y_stored, 16)

            sp.dma_start(k_sb[:, :], consts).then_inc(k_loaded, 16)
            load_rows(0)
            for dst, src in ((wk_sb, wk_rep), (bk_sb, bk_rep), (wq_raw, wq_stack),
                             (bv_sb, bv), (bo_sb, bo_rep)):
                sp.dma_start(dst[:, :], src).then_inc(w_loaded, 16)
            for dst, src in ((wv_sb, wv), (wo_sb, wo)):
                sp.dma_start(dst[:, :, :], src.rearrange("(h p) c -> p h c", p=P)).then_inc(w_loaded, 16)
            load_rows(1)
            stack_up(0, 0)

            def element(b, side, stat, nxt, out):
                if nxt:
                    stack_up(b + 1, side)
                load_cols(b)
                if stat:
                    load_rows(b + 2)
                if out:
                    store(b - 1)

            element(0, 1, True, True, False)
            with sp.Fori(1, B - 2) as b:
                element(b, (b + 1) % 2, True, True, True)
            element(B - 2, (B - 1) % 2, False, True, True)
            element(B - 1, 0, False, False, True)
            store(B - 1)
            sp.wait_ge(y_stored, 16 * B)

        @block.tensor
        def _(pe):
            def sum_rows(j):
                pe.wait_ge(xs_loaded, 16 * (j + 1))
                after(pe, t01_done, j)
                for ch in range(SC):
                    for hf in range(2):
                        k = 2 * ch + hf
                        mm = nc.tensor.matmul(bx[C * k:C * k + C, 0:CH], ones_m,
                                              xs[:, ch, 8 * hf:8 * hf + 8, :].rearrange("p m c -> p (m c)"),
                                              start=True, stop=True)
                mm.then_inc(part_mm, 1)

            def mean(j):
                pe.wait_ge(part_done, j + 1)
                for hf in range(2):
                    mm = nc.tensor.matmul(bx[:, 4 * hf:4 * hf + 4], k_sb[:, MEAN + P * hf:MEAN + P * hf + P],
                                          part[:, :], start=True, stop=True)
                mm.then_inc(mean_mm, 1)

            def gram_of(j):
                pe.wait_ge(mean_done, j + 1)
                pe.wait_ge(centred, j + 1)
                for t in range(T):
                    for ch in range(SC):
                        for q in range(Q):
                            mm = nc.tensor.matmul(bx[C * q:C * q + C, (C + 1) * t:(C + 1) * (t + 1)],
                                                  xc[:, ch, Q * t + q, 0:C], xc[:, ch, Q * t + q, :],
                                                  start=(ch == 0), stop=(ch == SC - 1))
                mm.then_inc(gram_mm, 1)

            def variance(j):
                pe.wait_ge(gram_done, j + 1)
                pe.wait_ge(trace_done, j + 1)
                nc.tensor.matmul(bx[:, 0:T], same_m, trace[:, :], start=True, stop=True).then_inc(var_mm, 1)

            def t_product(j, first, dst, done):
                pe.wait_ge(gblk_done, j + 1)
                if first == 0:
                    pe.wait_ge(vare_done, j + 1)
                else:
                    after(pe, yb_done, T * (j - 2))
                for i in range(2):
                    mm = nc.tensor.matmul(dst[:, CH * i:CH * i + CH],
                                          gblk[:, first + i].rearrange("p q c -> p (q c)"), wk_sb[:, :],
                                          start=True, stop=True)
                mm.then_inc(done, 1)

            def tb_product(j):
                pe.wait_ge(gblk_done, j + 1)
                after(pe, yb_done, T * (j - 2))
                nc.tensor.matmul(by[0:M, 0:CH], sblk[:, :, :].rearrange("p t q -> p (t q)"), wk_sb[:, :],
                                 start=True, stop=True).then_inc(tb_mm, 1)

            def score(b, p, side):
                pe.wait_ge(stacked, 16 * NSTACK * (b + 1))
                n = M * b + p
                after(pe, exped, n - NS + 1)
                settled(pe)
                for h in range(HC):
                    mm = nc.tensor.matmul(s_bank[p % NS][:, CH * h:CH * h + CH], wq_st[:, P * h:P * h + P],
                                          stack[:, side, p, :], start=True, stop=True)
                mm.then_inc(scores, 1)

            def column_sums(b, p):
                t, q = p // Q, p % Q
                pe.wait_ge(inverted, M * b + p + 1)
                if p == 0:
                    after(pe, acc_read, b)
                for h in range(HC):
                    mm = nc.tensor.matmul(acc[C * q:C * q + C, 0:CH], recip[:, t, q, h, :],
                                          e_sb[:, p % NS, h, :],
                                          start=(t == 0 and h == 0), stop=(t == T - 1 and h == HC - 1))
                mm.then_inc(summed, 1)

            def a_columns(j):
                pe.wait_ge(acc_read, j + 1)
                after(pe, tb_done, min(j + 3, B) if isinstance(j, int) else j + 3)
                for h in range(HC):
                    mm = nc.tensor.matmul(by[:, M * h:M * h + M], a_sb[:, P * h:P * h + P], pick_m,
                                          start=True, stop=True)
                mm.then_inc(a_mm, 1)

            def weights(j):
                pe.wait_ge(a_done, j + 1)
                pe.wait_ge(ws_done, j + 1)
                for h in range(HC):
                    for q in range(Q):
                        nc.tensor.matmul(by[C * q:C * q + C, 0:T * C], wv_sb[:, h, :], ws[:, h, :, q, :],
                                         start=(h == 0), stop=(h == HC - 1))
                for h in range(HC):
                    mm = nc.tensor.matmul(by[:, P:P + M], wobv[:, h].rearrange("p q c -> p (q c)"), aT[:, h, :],
                                          start=(h == 0), stop=(h == HC - 1))
                mm.then_inc(w_mm, 1)

            def y_product(j, first, dst, done):
                pe.wait_ge(wblk_done, j + 1)
                pe.wait_ge(wf_done, j + 1)
                pe.wait_ge(xcT_done, j + 1)
                if first:
                    after(pe, t23_done, min(j + 3, B) if isinstance(j, int) else j + 3)
                for i in range(2):
                    mm = nc.tensor.matmul(dst[:, S * i:S * i + S],
                                          wblk[:, first + i].rearrange("p q c -> p (q c)"), xcT[:, first + i, :],
                                          start=True, stop=True)
                mm.then_inc(done, 1)

            def element(b, side, stat, nxt, out, last=False):
                for p in range(M):
                    if p + AHEAD < M:
                        score(b, p + AHEAD, side)
                    elif nxt:
                        score(b + 1, p + AHEAD - M, 1 - side)
                    if p >= CLAG:
                        column_sums(b, p - CLAG)
                    elif out:
                        column_sums(b - 1, p - CLAG + M)
                    if nxt and p == 2:
                        t_product(b + 1, 0, bx, t01_mm)
                    if nxt and p == 3:
                        t_product(b + 1, 2, bz, t23_mm)
                    if nxt and p == 4:
                        tb_product(b + 1)
                    if stat and p == 5:
                        sum_rows(b + 2)
                    if out and p == 6:
                        a_columns(b - 1)
                    if stat and p == 7:
                        mean(b + 2)
                    if out and p == 9:
                        weights(b - 1)
                    if stat and p == 10:
                        gram_of(b + 2)
                    if out and p == 12:
                        y_product(b - 1, 0, by, y01_mm)
                    if out and p == 13:
                        y_product(b - 1, 2, bz, y23_mm)
                    if stat and p == 13:
                        variance(b + 2)

            def statistics(j):
                sum_rows(j)
                mean(j)
                gram_of(j)
                variance(j)

            pe.wait_ge(k_loaded, 16)
            pe.wait_ge(set_pool, 1)
            statistics(0)
            pe.wait_ge(w_loaded, 16 * 7)
            pe.wait_ge(set_dve, 2)
            t_product(0, 0, bx, t01_mm)
            t_product(0, 2, bz, t23_mm)
            tb_product(0)
            statistics(1)
            for p in range(AHEAD):
                score(0, p, 0)
            element(0, 0, True, True, False)
            with pe.Fori(1, B - 2) as b:
                element(b, b % 2, True, True, True)
            element(B - 2, (B - 2) % 2, False, True, True)
            element(B - 1, (B - 1) % 2, False, False, True)
            for p in range(M - CLAG, M):
                column_sums(B - 1, p)
            a_columns(B - 1)
            weights(B - 1)
            y_product(B - 1, 0, by, y01_mm)
            y_product(B - 1, 2, bz, y23_mm)

        @block.vector
        def _(dve):
            def sum_groups(j):
                dve.wait_ge(part_mm, j + 1)
                nc.vector.tensor_reduce(part[:, :], bx[:, 0:CH].rearrange("p (g e) -> p g e", g=G // 2),
                                        op=ALU.add, axis=AX.X).then_inc(part_done, 1)

            def read_mean(j):
                dve.wait_ge(mean_mm, j + 1)
                after(dve, centred, j)
                nc.vector.tensor_copy(nm[:, :], bx[:, 0:G])
                means = bx[:, 0:G].rearrange("p (t k) -> p t k", k=2)
                for k in range(2):
                    rows = slice(2 * C * k, 2 * C * (k + 1))
                    last = nc.vector.tensor_copy(nmT[rows, bass.ds(j, 1), :], means[rows, None, :, k])
                last.then_inc(mean_done, 1)

            def read_gram(j):
                dve.wait_ge(gram_mm, j + 1)
                after(dve, gblk_done, j)
                nc.vector.tensor_copy(gram[:, :, :].rearrange("p t c -> p (t c)"),
                                      bx[:, 0:T * (C + 1)]).then_inc(gram_done, 1)
                dve.wait_ge(diag_done, j + 1)
                nc.vector.tensor_reduce(trace[:, :], gdiag[:, :, :], op=ALU.add, axis=AX.X).then_inc(trace_done, 1)

            def read_variance(j):
                dve.wait_ge(var_mm, j + 1)
                nc.vector.tensor_scalar(vare[:, :], bx[:, 0:T], EPS, None, ALU.add).then_inc(vare_done, 1)
                dve.wait_ge(vare_done, j + 1)
                nc.vector.reciprocal(rs2[:, :], vare[:, :]).then_inc(var_done, 1)

            def read_t(j, first, src, ready, done):
                dve.wait_ge(ready, j + 1)
                dve.wait_ge(gblk_done, j + 1)
                after(dve, parts_done, j)
                for i in range(2):
                    last = nc.vector.scalar_tensor_tensor(t_sb[:, first + i, :], bk_sb[:, :],
                                                          ssum[:, first + i:first + i + 1],
                                                          src[:, CH * i:CH * i + CH], ALU.mult, ALU.add)
                last.then_inc(done, 1)

            def read_tb(j):
                dve.wait_ge(tb_mm, j + 1)
                after(dve, parts_done, j)
                nc.vector.tensor_tensor(tb_sb[:, :], by[0:M, 0:CH], bk_all[:, :], ALU.add).then_inc(tb_done, 1)

            def maximum(b, p):
                dve.wait_ge(scores, M * b + p + 1)
                nc.vector.tensor_reduce(negmax[:, p % NS, :],
                                        s_bank[p % NS][:, :].rearrange("p (h n) -> p h n", h=HC),
                                        op=ALU.max, axis=AX.X, negate=True).then_inc(maxed, 1)

            def invert(b, p):
                t, q = p // Q, p % Q
                dve.wait_ge(exped, M * b + p + 1)
                nc.vector.reciprocal(recip[:, t, q, :, t], rowsum[:, p % NS, :]).then_inc(inverted, 1)

            def read_acc(j):
                dve.wait_ge(summed, M * (j + 1))
                after(dve, a_mm, j)
                nc.vector.tensor_copy(a_sb[:, :], acc[:, 0:CH]).then_inc(acc_read, 1)

            def read_a(j):
                dve.wait_ge(a_mm, j + 1)
                after(dve, w_mm, j)
                nc.vector.tensor_copy(aT[:, :, :].rearrange("p h m -> p (h m)"),
                                      by[:, 0:HC * M]).then_inc(a_done, 1)

            def read_weights(j):
                dve.wait_ge(w_mm, j + 1)
                dve.wait_ge(rs_done, j + 1)
                after(dve, wblk_done, j)
                after(dve, yb_done, T * j)
                nc.vector.tensor_tensor(wf[:, :, :], by[:, 0:T * C].rearrange("p (t c) -> p t c", t=T),
                                        rs[:, bass.ds(j, 1), :].rearrange("p b t -> p (b t)")[:, :, None]
                                        .to_broadcast([P, T, C]), ALU.mult)
                for q in range(Q):
                    rows = slice(C * q, C * q + C)
                    bias = by[rows, P:P + M].rearrange("p (t q) -> p t q", q=Q)[:, :, q]
                    last = nc.vector.tensor_scalar(beff[rows, :], bias, bo_sb[rows, :], None, ALU.add)
                last.then_inc(wf_done, 1)

            def element(b, stat, nxt, out):
                for p in range(M):
                    maximum(b, p)
                    if p >= RLAG:
                        invert(b, p - RLAG)
                    elif out:
                        invert(b - 1, p - RLAG + M)
                    if out and p == 3:
                        read_acc(b - 1)
                    if nxt and p == 3:
                        read_t(b + 1, 0, bx, t01_mm, t01_done)
                    if nxt and p == 4:
                        read_t(b + 1, 2, bz, t23_mm, t23_done)
                    if nxt and p == 5:
                        read_tb(b + 1)
                    if stat and p == 6:
                        sum_groups(b + 2)
                    if out and p == 7:
                        read_a(b - 1)
                    if stat and p == 8:
                        read_mean(b + 2)
                    if out and p == 10:
                        read_weights(b - 1)
                    if stat and p == 11:
                        read_gram(b + 2)
                    if stat and p == 14:
                        read_variance(b + 2)

            def statistics(j):
                sum_groups(j)
                read_mean(j)
                read_gram(j)
                read_variance(j)

            dve.wait_ge(w_loaded, 16 * 7)
            dve.wait_ge(k_loaded, 16)
            nc.vector.tensor_copy(wq_hi[:, :], wq_raw[:, :]).then_inc(set_dve, 1)
            dve.wait_ge(set_dve, 1)
            nc.vector.scalar_tensor_tensor(wq_st[:, :], wq_hi[:, :].bitcast(f32), k_sb[0:ST, LOMASK:LOMASK + 1],
                                           wq_raw[:, :], ALU.mult, ALU.add).then_inc(set_dve, 1)
            dve.wait_ge(set_pool, 1)
            statistics(0)
            read_t(0, 0, bx, t01_mm, t01_done)
            read_t(0, 2, bz, t23_mm, t23_done)
            read_tb(0)
            statistics(1)
            element(0, True, True, False)
            with dve.Fori(1, B - 2) as b:
                element(b, True, True, True)
            element(B - 2, False, True, True)
            element(B - 1, False, False, True)
            for p in range(M - RLAG, M):
                invert(B - 1, p)
            read_acc(B - 1)
            read_a(B - 1)
            read_weights(B - 1)

        @block.scalar
        def _(act):
            def exponentials(b, p):
                n = M * b + p
                act.wait_ge(maxed, n + 1)
                after(act, summed, n - NS + 1)
                for h in range(HC):
                    last = nc.scalar.activation(e_sb[:, p % NS, h, :], s_bank[p % NS][:, CH * h:CH * h + CH],
                                                ACT.Exp, bias=negmax[:, p % NS, h:h + 1],
                                                accum_out=rowsum[:, p % NS, h:h + 1])
                last.then_inc(exped, 1)

            def read_y(j, first, src, ready):
                act.wait_ge(ready, j + 1)
                after(act, yo_done, j)
                for i in range(2):
                    nc.scalar.activation(yb[:, first + i, :], src[:, S * i:S * i + S], ACT.Identity,
                                         bias=beff[:, first + i:first + i + 1]).then_inc(yb_done, 1)

            def element(b, out):
                for p in range(M):
                    exponentials(b, p)
                    if out and p == 13:
                        read_y(b - 1, 0, by, y01_mm)
                    if out and p == 14:
                        read_y(b - 1, 2, bz, y23_mm)

            nc.scalar.preload_act_table(ACT.Exp)
            element(0, False)
            with act.Fori(1, B - 2) as b:
                element(b, True)
            element(B - 2, True)
            element(B - 1, True)
            read_y(B - 1, 0, by, y01_mm)
            read_y(B - 1, 2, bz, y23_mm)

        @block.gpsimd
        def _(pool):
            def centre_rows(j):
                pool.wait_ge(mean_done, j + 1)
                pool.wait_ge(xs_loaded, 16 * (j + 1))
                after(pool, gram_mm, j)
                for ch in range(SC):
                    shift = nm[:, :, None, None].to_broadcast([P, G, M // G, C])
                    last = nc.gpsimd.tensor_tensor(
                        xc[:, ch, :, 0:C].rearrange("p (g k) c -> p g k c", g=G),
                        xs[:, ch, :, :].rearrange("p (g k) c -> p g k c", g=G), shift, ALU.add)
                last.then_inc(centred, 1)

            def diagonal(j):
                pool.wait_ge(gram_done, j + 1)
                after(pool, trace_done, j)
                nc.gpsimd.tensor_tensor(gdiag[:, :, :], gram[:, :, 0:C],
                                        diag_m[:, None, :].to_broadcast([P, T, C]), ALU.mult
                                        ).then_inc(diag_done, 1)

            def blocks(j):
                pool.wait_ge(var_done, j + 1)
                nc.gpsimd.tensor_tensor(rs_now[:, :], vare[:, :], half[:, :], ALU.pow).then_inc(pool_step, 1)
                nc.gpsimd.tensor_tensor(gnorm[:, :, :], gram[:, :, 0:C],
                                        rs2[:, :, None].to_broadcast([P, T, C]), ALU.mult).then_inc(pool_step, 1)
                pool.wait_ge(pool_step, 3 * j + 2)
                after(pool, t01_mm, j)
                after(pool, t23_mm, j)
                after(pool, tb_mm, j)
                after(pool, t23_done, j)
                settled(pool)
                nc.gpsimd.tensor_tensor(ssum[:, :], gram[:, :, C], rs_now[:, :], ALU.mult).then_inc(pool_step, 1)
                nc.gpsimd.tensor_copy(rs[:, bass.ds(j, 1), :], rs_now[:, None, :]).then_inc(rs_done, 1)
                nc.gpsimd.tensor_tensor(gblk[:, :, :, :], gnorm[:, :, None, :].to_broadcast([P, T, Q, C]),
                                        own_m[:, None, :, None].to_broadcast([P, T, Q, C]), ALU.mult)
                pool.wait_ge(pool_step, 3 * j + 3)
                nc.gpsimd.tensor_tensor(sblk[:, :, :], ssum[:, :, None].to_broadcast([P, T, Q]),
                                        own_m[:, None, :].to_broadcast([P, T, Q]), ALU.mult).then_inc(gblk_done, 1)

            def parts(j):
                pool.wait_ge(t01_done, j + 1)
                pool.wait_ge(t23_done, j + 1)
                pool.wait_ge(tb_done, j + 1)
                after(pool, stacked, 16 * NSTACK * j)
                settled(pool)
                nc.gpsimd.tensor_copy(t_hi[:, :, :], t_sb[:, :, :])
                nc.gpsimd.tensor_copy(tb_hi[:, :], tb_sb[:, :]).then_inc(hi_done, 1)
                pool.wait_ge(hi_done, j + 1)
                nc.gpsimd.tensor_tensor(t_lo[:, :, :], t_sb[:, :, :], t_hi[:, :, :].bitcast(f32), ALU.subtract)
                nc.gpsimd.tensor_tensor(tb_lo[:, :], tb_sb[:, :], tb_hi[:, :].bitcast(f32), ALU.subtract
                                        ).then_inc(parts_done, 1)

            def centre_cols(j):
                pool.wait_ge(xT_loaded, 16 * (j + 1))
                pool.wait_ge(mean_done, j + 1)
                after(pool, y23_mm, j)
                settled(pool)
                shift = nmT[:, bass.ds(j, 1), :].rearrange("p b t -> p (b t)")[:, :, None].to_broadcast([P, T, S])
                nc.gpsimd.tensor_tensor(xcT[:, :, :], xT[:, bass.ds(j, 1), :, :].rearrange("p b t s -> p (b t) s"),
                                        shift, ALU.add).then_inc(xcT_done, 1)

            def scale_wo(j):
                pool.wait_ge(a_done, j + 1)
                after(pool, w_mm, j)
                nc.gpsimd.tensor_tensor(ws[:, :, :, :, :].rearrange("p h t q c -> p h (t q) c"),
                                        wo_sb[:, :, None, :].to_broadcast([P, HC, M, C]),
                                        aT[:, :, :, None].to_broadcast([P, HC, M, C]), ALU.mult
                                        ).then_inc(ws_done, 1)

            def weight_blocks(j):
                pool.wait_ge(wf_done, j + 1)
                after(pool, y23_mm, j)
                settled(pool)
                nc.gpsimd.tensor_tensor(wblk[:, :, :, :], wf[:, :, None, :].to_broadcast([P, T, Q, C]),
                                        own_m[:, None, :, None].to_broadcast([P, T, Q, C]), ALU.mult
                                        ).then_inc(wblk_done, 1)

            def residual(j):
                pool.wait_ge(yb_done, T * (j + 1))
                after(pool, y_stored, 16 * j)
                settled(pool)
                nc.gpsimd.tensor_tensor(yo[:, :, :], yb[:, :, :],
                                        xT[:, bass.ds(j, 1), :, :].rearrange("p b t s -> p (b t) s"), ALU.add
                                        ).then_inc(yo_done, 1)

            nc.gpsimd.memset(recip[:, :, :, :, :], 0.0)
            nc.gpsimd.memset(half[:, :], -0.5)
            nc.gpsimd.memset(xc[:, :, :, C:C + 1], 1.0)
            pool.wait_ge(w_loaded, 16 * 7)
            nc.gpsimd.tensor_scalar(bk_all[:, :], bk_sb[0:M, :], float(S), 0.0, ALU.mult, ALU.add)
            for h in range(HC):
                last = nc.gpsimd.tensor_scalar(wobv[:, h], wo_sb[:, h, None, :].to_broadcast([P, Q, C]),
                                               bv_sb[:, h:h + 1], 0.0, ALU.mult, ALU.add)
            last.then_inc(set_pool, 1)

            centre_rows(0)
            diagonal(0)
            blocks(0)
            parts(0)
            centre_rows(1)
            diagonal(1)
            blocks(1)

            def element(b, stat, nxt, out):
                if nxt:
                    parts(b + 1)
                if out:
                    centre_cols(b - 1)
                    scale_wo(b - 1)
                if stat:
                    centre_rows(b + 2)
                if out:
                    weight_blocks(b - 1)
                if stat:
                    diagonal(b + 2)
                    blocks(b + 2)
                if out:
                    residual(b - 1)

            element(0, True, True, False)
            with pool.Fori(1, B - 2) as b:
                element(b, True, True, True)
            element(B - 2, False, True, True)
            element(B - 1, False, False, True)
            centre_cols(B - 1)
            scale_wo(B - 1)
            weight_blocks(B - 1)
            residual(B - 1)


def kernel(x, L0_conv_Wq, L0_conv_bq, L0_conv_Wk, L0_conv_bk, L0_conv_Wv, L0_conv_bv, L0_conv_Wo, L0_conv_bo):
    import concourse.bacc as bacc
    from concourse.bass_utils import run_bass_kernel_spmd

    x, wq, bq, wk, bk, wv, bv, wo, bo = (np.asarray(a) for a in (
        x, L0_conv_Wq, L0_conv_bq, L0_conv_Wk, L0_conv_bk, L0_conv_Wv, L0_conv_bv, L0_conv_Wo, L0_conv_bo))
    arrays = {
        "x_rows": x.transpose(0, 1, 3, 2),
        "x_cols": x.transpose(0, 3, 2, 1).reshape(B, T, P, S),
        "wq_stack": np.concatenate([wq.T] * 3 + [bq[None]] * 3),
        "wk_rep": np.concatenate([wk.T] * Q),
        "bk_rep": np.broadcast_to(bk, (P, CH)),
        "wv": wv,
        "wo": wo.T,
        "bv": bv.reshape(HC, P).T,
        "bo_rep": np.tile(bo, Q)[:, None],
        "consts": shape_constants(),
    }
    arrays = {name: np.ascontiguousarray(a) for name, a in arrays.items()}
    nc = bacc.Bacc("TRN2", target_bir_lowering=False, num_devices=1)
    args = [nc.dram_tensor(name, a.shape, mybir.dt.from_np(a.dtype), kind="ExternalInput").ap()
            for name, a in arrays.items()]
    y = nc.dram_tensor("y_cols", (B, T, P, S), mybir.dt.float32, kind="ExternalOutput").ap()
    build(nc, *args, y)
    r = run_bass_kernel_spmd(nc, [arrays], core_ids=[0])
    return r.results[0]["y_cols"].reshape(B, M, C, S).transpose(0, 3, 2, 1)
```

```python
import numpy as np
from contextlib import ExitStack

import concourse.bass as bass
from concourse import mybir

B, S, C, M = 8, 256, 32, 16
CH = 256
G = 8
P = 128
Q = P // C
T = M // Q
SC = S // P
HC = CH // P
PER_GROUP = S * C * (M // G)
EPS = 1e-5
NP = 3
ST = NP * (C + 1)

DIAG = 0
SAME = DIAG + C
MEAN = SAME + P
PICK = MEAN + 2 * P
ONES = PICK + M
LOMASK = ONES + C
LOTB = LOMASK + 1
OWN = LOTB + 1
NCONST = OWN + Q


def shape_constants():
    p = np.arange(P)
    k = np.zeros((P, NCONST), np.float32)
    k[p, DIAG + p % C] = 1.0
    k[:, SAME:SAME + P] = (p[:, None] // (2 * C) == p[None, :] // (2 * C)) / PER_GROUP
    for hf in range(2):
        rows = (p // C) % 2 == hf
        k[rows, MEAN + hf * P:MEAN + (hf + 1) * P] = -1.0 / (PER_GROUP * C)
    for m in range(M):
        k[C * (m % Q) + m // Q, PICK + m] = 1.0
    k[:, ONES:ONES + C] = 1.0
    k[1:ST:NP, LOMASK] = -1.0
    k[2 * M:3 * M, LOTB] = -1.0
    k[p, OWN + p // C] = 1.0
    return k


def build(nc, x_rows, x_cols, wq_stack, wk_rep, bk_rep, wv, wo, bv, bo_rep, consts, y_cols):
    f32 = mybir.dt.float32
    f32r = mybir.dt.float32r
    ALU = mybir.AluOpType
    ACT = mybir.ActivationFunctionType
    AX = mybir.AxisListType

    NS = 4
    NE = 2 * Q
    AHEAD = 3
    NSTACK = Q + 1

    ctx = ExitStack()
    with ctx:
        def sb(name, shape, dt=f32):
            return ctx.enter_context(nc.sbuf_tensor(name, shape, dt))

        def bank(name):
            return ctx.enter_context(nc.psum_tensor(name, [P, 512], f32))

        def sem(name):
            return ctx.enter_context(nc.semaphore(name))

        k_sb = sb("k_sb", [P, NCONST])
        wq_raw = sb("wq_raw", [ST, CH])
        wq_hi = sb("wq_hi", [ST, CH], f32r)
        wq_st = sb("wq_st", [ST, CH], f32r)
        wk_sb = sb("wk_sb", [P, CH])
        bk_sb = sb("bk_sb", [P, CH])
        bk_all = sb("bk_all", [NP * M, CH])
        wv_sb = sb("wv_sb", [P, HC, C])
        wo_sb = sb("wo_sb", [P, HC, C])
        wobv = sb("wobv", [P, HC, Q, C])
        bv_sb = sb("bv_sb", [P, HC])
        bo_sb = sb("bo_sb", [P, 1])
        half = sb("half", [P, T])
        xs = sb("xs", [P, SC, M, C])
        xT = sb("xT", [P, B, T, S])
        xc = sb("xc", [P, SC, M, C + 1])
        xcT = sb("xcT", [P, T, S])
        part = sb("part", [P, G // 2])
        nm = sb("nm", [P, G])
        nmT = sb("nmT", [P, B, T])
        gram = sb("gram", [P, T, C + 1])
        gdiag = sb("gdiag", [P, T, C])
        trace = sb("trace", [P, T])
        vare = sb("vare", [P, T])
        rs2 = sb("rs2", [P, T])
        rs = sb("rs", [P, B, T])
        rs_now = sb("rs_now", [P, T])
        gnorm = sb("gnorm", [P, T, C])
        ssum = sb("ssum", [P, T])
        gblk = sb("gblk", [P, T, Q, C])
        sblk = sb("sblk", [P, NP, T, Q])
        t_sb = sb("t_sb", [P, T, CH])
        t_parts = sb("t_parts", [P, NP, T, CH], f32r)
        tb_sb = sb("tb_sb", [NP * M, CH])
        tb_hi = sb("tb_hi", [NP * M, CH], f32r)
        tb_parts = sb("tb_parts", [NP * M, CH], f32r)
        stack = sb("stack", [ST, 2, M, CH], f32r)
        negmax = sb("negmax", [P, NS, HC])
        rowsum = sb("rowsum", [P, NE // Q, Q, HC])
        e_sb = sb("e_sb", [P, NE, HC, CH])
        recip = sb("recip", [P, T, Q, HC, C])
        a_sb = sb("a_sb", [P, CH])
        aT = sb("aT", [P, HC, M])
        ws = sb("ws", [P, HC, T, Q, C])
        wf = sb("wf", [P, T, C])
        wblk = sb("wblk", [P, T, Q, C])
        beff = sb("beff", [P, T])
        yb = sb("yb", [P, T, S])
        yo = sb("yo", [P, T, S])

        s_bank = [bank(f"s_bank{i}") for i in range(NS)]
        acc = bank("acc")
        bx = bank("bx")
        by = bank("by")
        bz = bank("bz")

        k_loaded = sem("k_loaded")
        w_loaded = sem("w_loaded")
        xs_loaded = sem("xs_loaded")
        xT_loaded = sem("xT_loaded")
        set_pool = sem("set_pool")
        set_dve = sem("set_dve")
        part_mm = sem("part_mm")
        part_done = sem("part_done")
        mean_mm = sem("mean_mm")
        mean_done = sem("mean_done")
        centred = sem("centred")
        gram_mm = sem("gram_mm")
        gram_done = sem("gram_done")
        diag_done = sem("diag_done")
        trace_done = sem("trace_done")
        var_mm = sem("var_mm")
        vare_done = sem("vare_done")
        var_done = sem("var_done")
        rs_done = sem("rs_done")
        pool_step = sem("pool_step")
        gblk_done = sem("gblk_done")
        t01_mm = sem("t01_mm")
        t23_mm = sem("t23_mm")
        tb_mm = sem("tb_mm")
        t01_done = sem("t01_done")
        t23_done = sem("t23_done")
        tb_done = sem("tb_done")
        tb_hi_done = sem("tb_hi_done")
        hi_done = sem("hi_done")
        parts_done = sem("parts_done")
        stacked = sem("stacked")
        tb_parts_done = sem("tb_parts_done")
        scores = sem("scores")
        maxed = sem("maxed")
        exped = sem("exped")
        inverted = sem("inverted")
        summed = sem("summed")
        acc_read = sem("acc_read")
        a_mm = sem("a_mm")
        a_done = sem("a_done")
        ws_done = sem("ws_done")
        xcT_done = sem("xcT_done")
        w_mm = sem("w_mm")
        wf_done = sem("wf_done")
        wblk_done = sem("wblk_done")
        y01_mm = sem("y01_mm")
        y23_mm = sem("y23_mm")
        yb_done = sem("yb_done")
        yo_done = sem("yo_done")
        y_stored = sem("y_stored")

        def after(eng, s, count):
            if not (isinstance(count, int) and count <= 0):
                eng.wait_ge(s, count)

        def settled(eng):
            eng.nop(nofuse=True)

        diag_m = k_sb[:, DIAG:DIAG + C]
        same_m = k_sb[:, SAME:SAME + P]
        pick_m = k_sb[:, PICK:PICK + M]
        own_m = k_sb[:, OWN:OWN + Q]
        ones_m = k_sb[:, ONES:ONES + C]

        block = ctx.enter_context(nc.Block())

        @block.sync
        def _(sp):
            def load_rows(j):
                after(sp, centred, j)
                settled(sp)
                after(sp, part_mm, j)
                settled(sp)
                sp.dma_start(xs[:, :, :, :], x_rows[bass.ds(j, 1)].rearrange("b (h p) m c -> p (b h) m c", p=P)
                             ).then_inc(xs_loaded, 16)

            def load_cols(j):
                after(sp, xcT_done, j)
                settled(sp)
                sp.dma_start(xT[:, bass.ds(j, 1), :, :], x_cols[bass.ds(j, 1)].rearrange("b t p s -> p b t s")
                             ).then_inc(xT_loaded, 16)

            def stack_up(j, side):
                after(sp, scores, M * (j - 1))
                settled(sp)
                sp.wait_ge(hi_done, 2 * j + 2)
                settled(sp)
                sp.wait_ge(parts_done, j + 1)
                settled(sp)
                for q in range(Q):
                    sp.dma_start(stack[0:NP * C, side, q:M:Q, :].bitcast(f32),
                                 t_parts[C * q:C * q + C, :, :, :].bitcast(f32)).then_inc(stacked, 16)
                sp.wait_ge(tb_parts_done, j + 1)
                settled(sp)
                sp.dma_start(stack[NP * C:ST, side, :, :].bitcast(f32), tb_parts[:, :].bitcast(f32)
                             ).then_inc(stacked, 16)

            def store(j):
                sp.wait_ge(yo_done, j + 1)
                settled(sp)
                sp.dma_start(y_cols[bass.ds(j, 1)].rearrange("b t p s -> p b t s"), yo[:, None, :, :]
                             ).then_inc(y_stored, 16)

            sp.dma_start(k_sb[:, :], consts).then_inc(k_loaded, 16)
            load_rows(0)
            for dst, src in ((wk_sb, wk_rep), (bk_sb, bk_rep), (wq_raw, wq_stack),
                             (bv_sb, bv), (bo_sb, bo_rep)):
                sp.dma_start(dst[:, :], src).then_inc(w_loaded, 16)
            for dst, src in ((wv_sb, wv), (wo_sb, wo)):
                sp.dma_start(dst[:, :, :], src.rearrange("(h p) c -> p h c", p=P)).then_inc(w_loaded, 16)
            load_rows(1)
            stack_up(0, 0)

            def element(b, side, stat, nxt, out):
                if stat:
                    load_rows(b + 2)
                if nxt:
                    stack_up(b + 1, side)
                load_cols(b)
                if out:
                    store(b - 1)

            element(0, 1, True, True, False)
            with sp.Fori(1, B - 2) as b:
                element(b, (b + 1) % 2, True, True, True)
            element(B - 2, (B - 1) % 2, False, True, True)
            element(B - 1, 0, False, False, True)
            store(B - 1)
            sp.wait_ge(y_stored, 16 * B)

        @block.tensor
        def _(pe):
            def sum_rows(j):
                pe.wait_ge(xs_loaded, 16 * (j + 1))
                after(pe, t01_done, j)
                for ch in range(SC):
                    for hf in range(2):
                        k = 2 * ch + hf
                        mm = nc.tensor.matmul(bx[C * k:C * k + C, 0:CH], ones_m,
                                              xs[:, ch, 8 * hf:8 * hf + 8, :].rearrange("p m c -> p (m c)"),
                                              start=True, stop=True)
                mm.then_inc(part_mm, 1)

            def mean(j):
                pe.wait_ge(part_done, j + 1)
                for hf in range(2):
                    mm = nc.tensor.matmul(bx[:, 4 * hf:4 * hf + 4], k_sb[:, MEAN + P * hf:MEAN + P * hf + P],
                                          part[:, :], start=True, stop=True)
                mm.then_inc(mean_mm, 1)

            def gram_of(j):
                pe.wait_ge(mean_done, j + 1)
                pe.wait_ge(centred, j + 1)
                for t in range(T):
                    for ch in range(SC):
                        for q in range(Q):
                            mm = nc.tensor.matmul(bx[C * q:C * q + C, (C + 1) * t:(C + 1) * (t + 1)],
                                                  xc[:, ch, Q * t + q, 0:C], xc[:, ch, Q * t + q, :],
                                                  start=(ch == 0), stop=(ch == SC - 1))
                mm.then_inc(gram_mm, 1)

            def variance(j):
                pe.wait_ge(gram_done, j + 1)
                pe.wait_ge(trace_done, j + 1)
                nc.tensor.matmul(bx[:, 0:T], same_m, trace[:, :], start=True, stop=True).then_inc(var_mm, 1)

            def t_product(j, first, dst, done):
                pe.wait_ge(gblk_done, j + 1)
                if first == 0:
                    pe.wait_ge(vare_done, j + 1)
                for i in range(2):
                    mm = nc.tensor.matmul(dst[:, CH * i:CH * i + CH],
                                          gblk[:, first + i].rearrange("p q c -> p (q c)"), wk_sb[:, :],
                                          start=True, stop=True)
                mm.then_inc(done, 1)

            def tb_product(j):
                pe.wait_ge(gblk_done, j + 1)
                nc.tensor.matmul(by[0:NP * M, 0:CH], sblk[:, :, :, :].rearrange("p k t q -> p (k t q)"), wk_sb[:, :],
                                 start=True, stop=True).then_inc(tb_mm, 1)

            def score(b, p, side):
                pe.wait_ge(stacked, 16 * NSTACK * (b + 1))
                n = M * b + p
                after(pe, exped, n - NS + 1)
                settled(pe)
                for h in range(HC):
                    mm = nc.tensor.matmul(s_bank[p % NS][:, CH * h:CH * h + CH], wq_st[:, P * h:P * h + P],
                                          stack[:, side, p, :], start=True, stop=True)
                mm.then_inc(scores, 1)

            def column_sums(b, t):
                pe.wait_ge(inverted, T * b + t + 1)
                if t == 0:
                    after(pe, acc_read, b)
                for h in range(HC):
                    for q in range(Q):
                        mm = nc.tensor.matmul(acc[C * q:C * q + C, 0:CH], recip[:, t, q, h, :],
                                              e_sb[:, (Q * t + q) % NE, h, :],
                                              start=(t == 0 and h == 0), stop=(t == T - 1 and h == HC - 1))
                mm.then_inc(summed, 1)

            def a_columns(j):
                pe.wait_ge(acc_read, j + 1)
                after(pe, tb_done, min(j + 3, B) if isinstance(j, int) else j + 3)
                for h in range(HC):
                    mm = nc.tensor.matmul(by[:, M * h:M * h + M], a_sb[:, P * h:P * h + P], pick_m,
                                          start=True, stop=True)
                mm.then_inc(a_mm, 1)

            def weights(j):
                pe.wait_ge(a_done, j + 1)
                pe.wait_ge(ws_done, j + 1)
                for h in range(HC):
                    for q in range(Q):
                        nc.tensor.matmul(by[C * q:C * q + C, 0:T * C], wv_sb[:, h, :], ws[:, h, :, q, :],
                                         start=(h == 0), stop=(h == HC - 1))
                for h in range(HC):
                    mm = nc.tensor.matmul(by[:, P:P + M], wobv[:, h].rearrange("p q c -> p (q c)"), aT[:, h, :],
                                          start=(h == 0), stop=(h == HC - 1))
                mm.then_inc(w_mm, 1)

            def y_product(j, first, dst, done):
                pe.wait_ge(wblk_done, j + 1)
                pe.wait_ge(wf_done, j + 1)
                pe.wait_ge(xcT_done, j + 1)
                if first:
                    after(pe, t23_done, min(j + 3, B) if isinstance(j, int) else j + 3)
                for i in range(2):
                    mm = nc.tensor.matmul(dst[:, S * i:S * i + S],
                                          wblk[:, first + i].rearrange("p q c -> p (q c)"), xcT[:, first + i, :],
                                          start=True, stop=True)
                mm.then_inc(done, 1)

            def element(b, side, stat, nxt, out, last=False):
                for p in range(M):
                    if p + AHEAD < M:
                        score(b, p + AHEAD, side)
                    elif nxt:
                        score(b + 1, p + AHEAD - M, 1 - side)
                    if p % Q == 2 and p > Q:
                        column_sums(b, p // Q - 1)
                    elif p == 2 and out:
                        column_sums(b - 1, T - 1)
                    if nxt and p == 0:
                        t_product(b + 1, 0, bx, t01_mm)
                    if nxt and p == 1:
                        t_product(b + 1, 2, bz, t23_mm)
                    if nxt and p == 3:
                        tb_product(b + 1)
                    if stat and p == 5:
                        sum_rows(b + 2)
                    if out and p == 6:
                        a_columns(b - 1)
                    if stat and p == 7:
                        mean(b + 2)
                    if out and p == 9:
                        weights(b - 1)
                    if stat and p == 10:
                        gram_of(b + 2)
                    if out and p == 12:
                        y_product(b - 1, 0, by, y01_mm)
                    if out and p == 13:
                        y_product(b - 1, 2, bz, y23_mm)
                    if stat and p == 13:
                        variance(b + 2)

            def statistics(j):
                sum_rows(j)
                mean(j)
                gram_of(j)
                variance(j)

            pe.wait_ge(k_loaded, 16)
            pe.wait_ge(set_pool, 1)
            statistics(0)
            pe.wait_ge(w_loaded, 16 * 7)
            pe.wait_ge(set_dve, 2)
            t_product(0, 0, bx, t01_mm)
            t_product(0, 2, bz, t23_mm)
            tb_product(0)
            statistics(1)
            for p in range(AHEAD):
                score(0, p, 0)
            element(0, 0, True, True, False)
            with pe.Fori(1, B - 2) as b:
                element(b, b % 2, True, True, True)
            element(B - 2, (B - 2) % 2, False, True, True)
            element(B - 1, (B - 1) % 2, False, False, True)
            column_sums(B - 1, T - 1)
            a_columns(B - 1)
            weights(B - 1)
            y_product(B - 1, 0, by, y01_mm)
            y_product(B - 1, 2, bz, y23_mm)

        @block.vector
        def _(dve):
            def sum_groups(j):
                dve.wait_ge(part_mm, j + 1)
                nc.vector.tensor_reduce(part[:, :], bx[:, 0:CH].rearrange("p (g e) -> p g e", g=G // 2),
                                        op=ALU.add, axis=AX.X).then_inc(part_done, 1)

            def read_mean(j):
                dve.wait_ge(mean_mm, j + 1)
                after(dve, centred, j)
                nc.vector.tensor_copy(nm[:, :], bx[:, 0:G])
                means = bx[:, 0:G].rearrange("p (t k) -> p t k", k=2)
                for k in range(2):
                    rows = slice(2 * C * k, 2 * C * (k + 1))
                    last = nc.vector.tensor_copy(nmT[rows, bass.ds(j, 1), :], means[rows, None, :, k])
                last.then_inc(mean_done, 1)

            def read_gram(j):
                dve.wait_ge(gram_mm, j + 1)
                after(dve, gblk_done, j)
                nc.vector.tensor_copy(gram[:, :, :].rearrange("p t c -> p (t c)"),
                                      bx[:, 0:T * (C + 1)]).then_inc(gram_done, 1)
                dve.wait_ge(diag_done, j + 1)
                nc.vector.tensor_reduce(trace[:, :], gdiag[:, :, :], op=ALU.add, axis=AX.X).then_inc(trace_done, 1)

            def read_variance(j):
                dve.wait_ge(var_mm, j + 1)
                nc.vector.tensor_scalar(vare[:, :], bx[:, 0:T], EPS, None, ALU.add).then_inc(vare_done, 1)
                dve.wait_ge(vare_done, j + 1)
                nc.vector.reciprocal(rs2[:, :], vare[:, :]).then_inc(var_done, 1)

            def read_t(j, first, src, ready, done):
                dve.wait_ge(ready, j + 1)
                dve.wait_ge(gblk_done, j + 1)
                after(dve, parts_done, j)
                for i in range(2):
                    last = nc.vector.scalar_tensor_tensor(t_sb[:, first + i, :], bk_sb[:, :],
                                                          ssum[:, first + i:first + i + 1],
                                                          src[:, CH * i:CH * i + CH], ALU.mult, ALU.add)
                last.then_inc(done, 1)

            def read_tb(j):
                dve.wait_ge(tb_mm, j + 1)
                after(dve, stacked, 16 * NSTACK * j)
                nc.vector.tensor_tensor(tb_sb[:, :], by[0:NP * M, 0:CH], bk_all[:, :], ALU.add).then_inc(tb_done, 1)
                dve.wait_ge(tb_done, j + 1)
                nc.vector.tensor_copy(tb_hi[:, :], tb_sb[:, :]).then_inc(tb_hi_done, 1)
                dve.wait_ge(tb_hi_done, j + 1)
                nc.vector.scalar_tensor_tensor(tb_parts[:, :], tb_hi[:, :].bitcast(f32),
                                               k_sb[0:NP * M, LOTB:LOTB + 1], tb_sb[:, :], ALU.mult, ALU.add
                                               ).then_inc(tb_parts_done, 1)

            def high_part(j):
                dve.wait_ge(t23_done, j + 1)
                after(dve, stacked, 16 * NSTACK * j)
                for k in range(2):
                    nc.vector.tensor_copy(t_parts[:, k].rearrange("p t n -> p (t n)"),
                                          t_sb[:, :, :].rearrange("p t n -> p (t n)")).then_inc(hi_done, 1)

            def maximum(b, p):
                dve.wait_ge(scores, M * b + p + 1)
                nc.vector.tensor_reduce(negmax[:, p % NS, :],
                                        s_bank[p % NS][:, :].rearrange("p (h n) -> p h n", h=HC),
                                        op=ALU.max, axis=AX.X, negate=True).then_inc(maxed, 1)

            def invert(b, t):
                dve.wait_ge(exped, M * b + Q * (t + 1))
                nc.vector.reciprocal(recip[:, t, :, :, t], rowsum[:, t % 2, :, :]).then_inc(inverted, 1)

            def read_acc(j):
                dve.wait_ge(summed, T * (j + 1))
                after(dve, a_mm, j)
                nc.vector.tensor_copy(a_sb[:, :], acc[:, 0:CH]).then_inc(acc_read, 1)

            def read_a(j):
                dve.wait_ge(a_mm, j + 1)
                after(dve, w_mm, j)
                nc.vector.tensor_copy(aT[:, :, :].rearrange("p h m -> p (h m)"),
                                      by[:, 0:HC * M]).then_inc(a_done, 1)

            def read_weights(j):
                dve.wait_ge(w_mm, j + 1)
                dve.wait_ge(rs_done, j + 1)
                after(dve, wblk_done, j)
                after(dve, yb_done, T * j)
                nc.vector.tensor_tensor(wf[:, :, :], by[:, 0:T * C].rearrange("p (t c) -> p t c", t=T),
                                        rs[:, bass.ds(j, 1), :].rearrange("p b t -> p (b t)")[:, :, None]
                                        .to_broadcast([P, T, C]), ALU.mult)
                for q in range(Q):
                    rows = slice(C * q, C * q + C)
                    bias = by[rows, P:P + M].rearrange("p (t q) -> p t q", q=Q)[:, :, q]
                    last = nc.vector.tensor_scalar(beff[rows, :], bias, bo_sb[rows, :], None, ALU.add)
                last.then_inc(wf_done, 1)

            def element(b, stat, nxt, out):
                for p in range(M):
                    maximum(b, p)
                    if p % Q == 1 and p > Q:
                        invert(b, p // Q - 1)
                    elif p == 1 and out:
                        invert(b - 1, T - 1)
                    if out and p == 3:
                        read_acc(b - 1)
                    if nxt and p == 1:
                        read_t(b + 1, 0, bx, t01_mm, t01_done)
                    if nxt and p == 2:
                        read_t(b + 1, 2, bz, t23_mm, t23_done)
                    if nxt and p == 4:
                        high_part(b + 1)
                    if nxt and p == 5:
                        read_tb(b + 1)
                    if stat and p == 6:
                        sum_groups(b + 2)
                    if out and p == 7:
                        read_a(b - 1)
                    if stat and p == 8:
                        read_mean(b + 2)
                    if out and p == 10:
                        read_weights(b - 1)
                    if stat and p == 11:
                        read_gram(b + 2)
                    if stat and p == 14:
                        read_variance(b + 2)

            def statistics(j):
                sum_groups(j)
                read_mean(j)
                read_gram(j)
                read_variance(j)

            dve.wait_ge(w_loaded, 16 * 7)
            dve.wait_ge(k_loaded, 16)
            nc.vector.tensor_copy(wq_hi[:, :], wq_raw[:, :]).then_inc(set_dve, 1)
            dve.wait_ge(set_dve, 1)
            nc.vector.scalar_tensor_tensor(wq_st[:, :], wq_hi[:, :].bitcast(f32), k_sb[0:ST, LOMASK:LOMASK + 1],
                                           wq_raw[:, :], ALU.mult, ALU.add).then_inc(set_dve, 1)
            dve.wait_ge(set_pool, 1)
            statistics(0)
            read_t(0, 0, bx, t01_mm, t01_done)
            read_t(0, 2, bz, t23_mm, t23_done)
            high_part(0)
            read_tb(0)
            statistics(1)
            element(0, True, True, False)
            with dve.Fori(1, B - 2) as b:
                element(b, True, True, True)
            element(B - 2, False, True, True)
            element(B - 1, False, False, True)
            invert(B - 1, T - 1)
            read_acc(B - 1)
            read_a(B - 1)
            read_weights(B - 1)

        @block.scalar
        def _(act):
            def exponentials(b, p):
                n = M * b + p
                act.wait_ge(maxed, n + 1)
                if p % Q == 0:
                    after(act, summed, T * b + p // Q - 1)
                for h in range(HC):
                    last = nc.scalar.activation(e_sb[:, p % NE, h, :], s_bank[p % NS][:, CH * h:CH * h + CH],
                                                ACT.Exp, bias=negmax[:, p % NS, h:h + 1],
                                                accum_out=rowsum[:, p // Q % 2, p % Q, h:h + 1])
                last.then_inc(exped, 1)

            def read_y(j, first, src, ready):
                act.wait_ge(ready, j + 1)
                after(act, yo_done, j)
                for i in range(2):
                    nc.scalar.activation(yb[:, first + i, :], src[:, S * i:S * i + S], ACT.Identity,
                                         bias=beff[:, first + i:first + i + 1]).then_inc(yb_done, 1)

            def element(b, out):
                for p in range(M):
                    exponentials(b, p)
                    if out and p == 13:
                        read_y(b - 1, 0, by, y01_mm)
                    if out and p == 14:
                        read_y(b - 1, 2, bz, y23_mm)

            nc.scalar.preload_act_table(ACT.Exp)
            element(0, False)
            with act.Fori(1, B - 2) as b:
                element(b, True)
            element(B - 2, True)
            element(B - 1, True)
            read_y(B - 1, 0, by, y01_mm)
            read_y(B - 1, 2, bz, y23_mm)

        @block.gpsimd
        def _(pool):
            def centre_rows(j):
                pool.wait_ge(mean_done, j + 1)
                pool.wait_ge(xs_loaded, 16 * (j + 1))
                after(pool, gram_mm, j)
                for ch in range(SC):
                    shift = nm[:, :, None, None].to_broadcast([P, G, M // G, C])
                    last = nc.gpsimd.tensor_tensor(
                        xc[:, ch, :, 0:C].rearrange("p (g k) c -> p g k c", g=G),
                        xs[:, ch, :, :].rearrange("p (g k) c -> p g k c", g=G), shift, ALU.add)
                last.then_inc(centred, 1)

            def diagonal(j):
                pool.wait_ge(gram_done, j + 1)
                after(pool, trace_done, j)
                nc.gpsimd.tensor_tensor(gdiag[:, :, :], gram[:, :, 0:C],
                                        diag_m[:, None, :].to_broadcast([P, T, C]), ALU.mult
                                        ).then_inc(diag_done, 1)

            def blocks(j):
                pool.wait_ge(var_done, j + 1)
                nc.gpsimd.tensor_tensor(rs_now[:, :], vare[:, :], half[:, :], ALU.pow).then_inc(pool_step, 1)
                nc.gpsimd.tensor_tensor(gnorm[:, :, :], gram[:, :, 0:C],
                                        rs2[:, :, None].to_broadcast([P, T, C]), ALU.mult).then_inc(pool_step, 1)
                pool.wait_ge(pool_step, 3 * j + 2)
                after(pool, t01_mm, j)
                after(pool, t23_mm, j)
                after(pool, tb_mm, j)
                after(pool, t23_done, j)
                settled(pool)
                nc.gpsimd.tensor_tensor(ssum[:, :], gram[:, :, C], rs_now[:, :], ALU.mult).then_inc(pool_step, 1)
                nc.gpsimd.tensor_copy(rs[:, bass.ds(j, 1), :], rs_now[:, None, :]).then_inc(rs_done, 1)
                nc.gpsimd.tensor_tensor(gblk[:, :, :, :], gnorm[:, :, None, :].to_broadcast([P, T, Q, C]),
                                        own_m[:, None, :, None].to_broadcast([P, T, Q, C]), ALU.mult)
                pool.wait_ge(pool_step, 3 * j + 3)
                nc.gpsimd.tensor_tensor(sblk[:, :, :, :], ssum[:, None, :, None].to_broadcast([P, NP, T, Q]),
                                        own_m[:, None, None, :].to_broadcast([P, NP, T, Q]), ALU.mult
                                        ).then_inc(gblk_done, 1)

            def low_part(j):
                pool.wait_ge(hi_done, 2 * j + 1)
                nc.gpsimd.tensor_tensor(t_parts[:, 2], t_sb[:, :, :], t_parts[:, 0].bitcast(f32), ALU.subtract
                                        ).then_inc(parts_done, 1)

            def centre_cols(j):
                pool.wait_ge(xT_loaded, 16 * (j + 1))
                pool.wait_ge(mean_done, j + 1)
                after(pool, y23_mm, j)
                settled(pool)
                shift = nmT[:, bass.ds(j, 1), :].rearrange("p b t -> p (b t)")[:, :, None].to_broadcast([P, T, S])
                nc.gpsimd.tensor_tensor(xcT[:, :, :], xT[:, bass.ds(j, 1), :, :].rearrange("p b t s -> p (b t) s"),
                                        shift, ALU.add).then_inc(xcT_done, 1)

            def scale_wo(j):
                pool.wait_ge(a_done, j + 1)
                after(pool, w_mm, j)
                nc.gpsimd.tensor_tensor(ws[:, :, :, :, :].rearrange("p h t q c -> p h (t q) c"),
                                        wo_sb[:, :, None, :].to_broadcast([P, HC, M, C]),
                                        aT[:, :, :, None].to_broadcast([P, HC, M, C]), ALU.mult
                                        ).then_inc(ws_done, 1)

            def weight_blocks(j):
                pool.wait_ge(wf_done, j + 1)
                after(pool, y23_mm, j)
                settled(pool)
                nc.gpsimd.tensor_tensor(wblk[:, :, :, :], wf[:, :, None, :].to_broadcast([P, T, Q, C]),
                                        own_m[:, None, :, None].to_broadcast([P, T, Q, C]), ALU.mult
                                        ).then_inc(wblk_done, 1)

            def residual(j):
                pool.wait_ge(yb_done, T * (j + 1))
                after(pool, y_stored, 16 * j)
                settled(pool)
                nc.gpsimd.tensor_tensor(yo[:, :, :], yb[:, :, :],
                                        xT[:, bass.ds(j, 1), :, :].rearrange("p b t s -> p (b t) s"), ALU.add
                                        ).then_inc(yo_done, 1)

            nc.gpsimd.memset(recip[:, :, :, :, :], 0.0)
            nc.gpsimd.memset(half[:, :], -0.5)
            nc.gpsimd.memset(xc[:, :, :, C:C + 1], 1.0)
            pool.wait_ge(w_loaded, 16 * 7)
            nc.gpsimd.tensor_scalar(bk_all[:, :], bk_sb[0:NP * M, :], float(S), 0.0, ALU.mult, ALU.add)
            for h in range(HC):
                last = nc.gpsimd.tensor_scalar(wobv[:, h], wo_sb[:, h, None, :].to_broadcast([P, Q, C]),
                                               bv_sb[:, h:h + 1], 0.0, ALU.mult, ALU.add)
            last.then_inc(set_pool, 1)

            centre_rows(0)
            diagonal(0)
            blocks(0)
            low_part(0)
            centre_rows(1)
            diagonal(1)
            blocks(1)

            def element(b, stat, nxt, out):
                if nxt:
                    low_part(b + 1)
                if out:
                    centre_cols(b - 1)
                    scale_wo(b - 1)
                if stat:
                    centre_rows(b + 2)
                if out:
                    weight_blocks(b - 1)
                if stat:
                    diagonal(b + 2)
                    blocks(b + 2)
                if out:
                    residual(b - 1)

            element(0, True, True, False)
            with pool.Fori(1, B - 2) as b:
                element(b, True, True, True)
            element(B - 2, False, True, True)
            element(B - 1, False, False, True)
            centre_cols(B - 1)
            scale_wo(B - 1)
            weight_blocks(B - 1)
            residual(B - 1)


def kernel(x, L0_conv_Wq, L0_conv_bq, L0_conv_Wk, L0_conv_bk, L0_conv_Wv, L0_conv_bv, L0_conv_Wo, L0_conv_bo):
    import concourse.bacc as bacc
    from concourse.bass_utils import run_bass_kernel_spmd

    x, wq, bq, wk, bk, wv, bv, wo, bo = (np.asarray(a) for a in (
        x, L0_conv_Wq, L0_conv_bq, L0_conv_Wk, L0_conv_bk, L0_conv_Wv, L0_conv_bv, L0_conv_Wo, L0_conv_bo))
    arrays = {
        "x_rows": x.transpose(0, 1, 3, 2),
        "x_cols": x.transpose(0, 3, 2, 1).reshape(B, T, P, S),
        "wq_stack": np.repeat(np.concatenate([wq.T, bq[None]]), NP, axis=0),
        "wk_rep": np.concatenate([wk.T] * Q),
        "bk_rep": np.broadcast_to(bk, (P, CH)),
        "wv": wv,
        "wo": wo.T,
        "bv": bv.reshape(HC, P).T,
        "bo_rep": np.tile(bo, Q)[:, None],
        "consts": shape_constants(),
    }
    arrays = {name: np.ascontiguousarray(a) for name, a in arrays.items()}
    nc = bacc.Bacc("TRN2", target_bir_lowering=False, num_devices=1)
    args = [nc.dram_tensor(name, a.shape, mybir.dt.from_np(a.dtype), kind="ExternalInput").ap()
            for name, a in arrays.items()]
    y = nc.dram_tensor("y_cols", (B, T, P, S), mybir.dt.float32, kind="ExternalOutput").ap()
    build(nc, *args, y)
    r = run_bass_kernel_spmd(nc, [arrays], core_ids=[0])
    return r.results[0]["y_cols"].reshape(B, M, C, S).transpose(0, 3, 2, 1)
```

```python
import numpy as np
from contextlib import ExitStack

import concourse.bass as bass
from concourse import mybir

B, S, C, M = 8, 256, 32, 16
CH = 256
G = 8
P = 128
Q = P // C
T = M // Q
SC = S // P
HC = CH // P
PER_GROUP = S * C * (M // G)
EPS = 1e-5
NP = 3
ST = NP * (C + 1)

DIAG = 0
SAME = DIAG + C
MEAN = SAME + P
PICK = MEAN + 2 * P
ONES = PICK + M
LOMASK = ONES + C
OWN = LOMASK + 1
NCONST = OWN + Q

STEADY = dict(
    t01_product=0, t23_product=2, tb_product=1, gram=4, variance=8, sum_rows=10, mean=14, column_sums=1,
    a_columns=5, weights=12, y01_product=4, y23_product=7,
    read_t01=2, read_t23=4, high_part=5, read_tb=3, read_mean=2, read_gram=5, sum_diagonal=6,
    read_variance=10, sum_groups=13, invert=1, read_acc=3, read_a=7, read_weights=14, read_y23=10,
    read_y01=6,
)
FIRST = dict(
    t01_product=3, t23_product=5, tb_product=3, gram=7, variance=10, sum_rows=10, mean=10, column_sums=0,
    sum_rows_2=2, mean_2=3,
    read_t01=4, read_t23=7, high_part=7, read_tb=6, read_gram=7, sum_diagonal=7, read_variance=10,
    sum_groups=11, invert=0, read_y23=9, sum_groups_2=2, read_mean_2=4,
)
LAST = dict(
    column_sums=0, a_columns=3, weights=8, y01_product=2, y23_product=6,
    invert=0, read_acc=3, read_a=5, read_weights=11, read_y23=10,
    read_y01=8,
)


def shape_constants():
    p = np.arange(P)
    k = np.zeros((P, NCONST), np.float32)
    k[p, DIAG + p % C] = 1.0
    k[:, SAME:SAME + P] = (p[:, None] // (2 * C) == p[None, :] // (2 * C)) / PER_GROUP
    for hf in range(2):
        rows = (p // C) % 2 == hf
        k[rows, MEAN + hf * P:MEAN + (hf + 1) * P] = -1.0 / (PER_GROUP * C)
    for m in range(M):
        k[C * (m % Q) + m // Q, PICK + m] = 1.0
    k[:, ONES:ONES + C] = 1.0
    k[1:2 * C:2, LOMASK] = -1.0
    k[NP * C + 1, LOMASK] = -1.0
    k[p, OWN + p // C] = 1.0
    return k


def build(nc, x_rows, x_cols, wq_stack, wk_rep, bk_rep, wv, wo, bv, bo_rep, consts, y_cols):
    f32 = mybir.dt.float32
    f32r = mybir.dt.float32r
    ALU = mybir.AluOpType
    ACT = mybir.ActivationFunctionType
    AX = mybir.AxisListType

    NS = 4
    NE = 2 * Q
    LEAD = 1
    AHEAD = 3

    ctx = ExitStack()
    with ctx:
        def sb(name, shape, dt=f32):
            return ctx.enter_context(nc.sbuf_tensor(name, shape, dt))

        def bank(name):
            return ctx.enter_context(nc.psum_tensor(name, [P, 512], f32))

        def sem(name):
            return ctx.enter_context(nc.semaphore(name))

        k_sb = sb("k_sb", [P, NCONST])
        wq_raw = sb("wq_raw", [ST, CH])
        wq_hi = sb("wq_hi", [ST, CH], f32r)
        wq_st = sb("wq_st", [ST, CH], f32r)
        wk_sb = sb("wk_sb", [P, CH])
        bk_sb = sb("bk_sb", [P, CH])
        wv_sb = sb("wv_sb", [P, HC, C])
        wo_sb = sb("wo_sb", [P, HC, C])
        wobv = sb("wobv", [P, HC, Q, C])
        bv_sb = sb("bv_sb", [P, HC])
        bo_sb = sb("bo_sb", [P, 1])
        rows_all = sb("rows_all", [P, 1])
        half = sb("half", [P, T])
        xs = sb("xs", [P, SC, M, C])
        xs_second = sb("xs_second", [P, SC, M, C])
        xT = sb("xT", [P, T, S])
        xc = sb("xc", [P, SC, M, C + 1])
        xcT = sb("xcT", [P, 2, T, S])
        part = sb("part", [P, G // 2])
        nm = sb("nm", [P, G])
        nmT = sb("nmT", [P, B, T])
        gram = sb("gram", [P, T, C + 1])
        gdiag = sb("gdiag", [P, T, C])
        trace = sb("trace", [P, T])
        vare = sb("vare", [P, T])
        rs2 = sb("rs2", [P, T])
        rs = sb("rs", [P, B, T])
        rs_now = sb("rs_now", [P, T])
        gnorm = sb("gnorm", [P, T, C])
        ssum = sb("ssum", [P, T])
        gblk = sb("gblk", [P, T, Q, C])
        sblk = sb("sblk", [P, 2, Q, T])
        t_sb = sb("t_sb", [P, T + 1, CH])
        t_parts = sb("t_parts", [P, 2, T + 1, CH], f32r)
        stack = sb("stack", [ST, 2, Q, T, CH], f32r)
        negmax = sb("negmax", [P, NS, HC])
        rowsum = sb("rowsum", [P, NE // Q, Q, HC])
        e_sb = sb("e_sb", [P, NE, HC, CH])
        recip = sb("recip", [P, T, Q, HC, C])
        a_sb = sb("a_sb", [P, CH])
        aT = sb("aT", [P, HC, M])
        ws = sb("ws", [P, HC, T, Q, C])
        wn = sb("wn", [P, T, C])
        wf = sb("wf", [P, T, C])
        wblk = sb("wblk", [P, T, Q, C])
        beff = sb("beff", [P, T])
        yb = sb("yb", [P, T, S])
        yb_end = sb("yb_end", [P, T, S])

        s_bank = [bank(f"s_bank{i}") for i in range(NS)]
        acc = bank("acc")
        bx = bank("bx")
        by = bank("by")
        bz = bank("bz")

        k_loaded = sem("k_loaded")
        w_loaded = sem("w_loaded")
        xs_loaded = sem("xs_loaded")
        second_loaded = sem("second_loaded")
        xT_loaded = sem("xT_loaded")
        set_zeros = sem("set_zeros")
        set_pool = sem("set_pool")
        set_dve = sem("set_dve")
        part_mm = sem("part_mm")
        part_done = sem("part_done")
        mean_mm = sem("mean_mm")
        mean_done = sem("mean_done")
        centred = sem("centred")
        centred_by_dve = sem("centred_by_dve")
        gram_mm = sem("gram_mm")
        gram_done = sem("gram_done")
        diag_done = sem("diag_done")
        trace_done = sem("trace_done")
        var_mm = sem("var_mm")
        vare_done = sem("vare_done")
        var_done = sem("var_done")
        rs_done = sem("rs_done")
        gnorm_done = sem("gnorm_done")
        std_done = sem("std_done")
        ssum_done = sem("ssum_done")
        gblk_done = sem("gblk_done")
        sblk_done = sem("sblk_done")
        t01_mm = sem("t01_mm")
        t23_mm = sem("t23_mm")
        tb_mm = sem("tb_mm")
        t01_done = sem("t01_done")
        t23_done = sem("t23_done")
        tb_done = sem("tb_done")
        hi_done = sem("hi_done")
        parts_done = sem("parts_done")
        stacked = [sem(f"stacked{q}") for q in range(Q)]
        bias_stacked = sem("bias_stacked")
        scores = sem("scores")
        maxed = sem("maxed")
        exped = sem("exped")
        inverted = sem("inverted")
        summed = sem("summed")
        acc_read = sem("acc_read")
        a_mm = sem("a_mm")
        a_done = sem("a_done")
        ws_done = sem("ws_done")
        xcT_done = sem("xcT_done")
        w_mm = sem("w_mm")
        wn_done = sem("wn_done")
        wf_done = sem("wf_done")
        beff_done = sem("beff_done")
        wblk_done = sem("wblk_done")
        y01_mm = sem("y01_mm")
        y23_mm = sem("y23_mm")
        y01_read = sem("y01_read")
        y23_read = sem("y23_read")
        y_stored = sem("y_stored")

        def after(eng, s, count):
            if not (isinstance(count, int) and count <= 0):
                eng.wait_ge(s, count)

        def rows_of(eng, j):
            if isinstance(j, int) and j == 1:
                eng.wait_ge(second_loaded, 16)
                return xs_second
            eng.wait_ge(xs_loaded, 16 if isinstance(j, int) and j == 0 else 16 * j)
            return xs

        def settled(eng):
            eng.nop(nofuse=True)

        diag_m = k_sb[:, DIAG:DIAG + C]
        same_m = k_sb[:, SAME:SAME + P]
        pick_m = k_sb[:, PICK:PICK + M]
        own_m = k_sb[:, OWN:OWN + Q]
        ones_m = k_sb[:, ONES:ONES + C]

        def slots(first, last):
            return FIRST if first else LAST if last else STEADY

        block = ctx.enter_context(nc.Block())

        @block.sync
        def _(sp):
            def load_rows(j, dst, loaded):
                sp.dma_start(dst[:, :, :, :], x_rows[bass.ds(j, 1)].rearrange("b (h p) m c -> p (b h) m c", p=P)
                             ).then_inc(loaded, 16)

            def load_next_rows(j):
                sp.wait_ge(centred, j)
                settled(sp)
                sp.wait_ge(part_mm, j)
                settled(sp)
                load_rows(j, xs, xs_loaded)

            def load_cols(j):
                after(sp, xcT_done, j)
                settled(sp)
                sp.dma_start(xT[:, None, :, :], x_cols[bass.ds(j, 1)].rearrange("b t p s -> p b t s")
                             ).then_inc(xT_loaded, 16)

            def stack_up(j, side, first=False):
                after(sp, scores, M * (j - 1))
                settled(sp)
                sp.wait_ge(hi_done, j + 1)
                settled(sp)

                def high(q):
                    part = t_parts[C * q:C * q + C, 0, None, 0:T, :].to_broadcast([C, 2, T, CH])
                    sp.dma_start(stack[0:2 * C, side, q, :, :].bitcast(f32), part.bitcast(f32)
                                 ).then_inc(stacked[q], 16)

                def low(q):
                    sp.dma_start(stack[2 * C:3 * C, side, q, :, :].bitcast(f32),
                                 t_parts[C * q:C * q + C, 1, 0:T, :].bitcast(f32)).then_inc(stacked[q], 16)

                def bias(part):
                    dst = stack[NP * C:NP * C + 2, side] if part == 0 else stack[NP * C + 2:ST, side]
                    src = t_parts[0:2 * M, 0, T, :] if part == 0 else t_parts[0:M, 1, T, :]
                    sp.dma_start(dst.bitcast(f32), src.bitcast(f32)).then_inc(bias_stacked, 16)

                if first:
                    high(0)
                    bias(0)
                    sp.wait_ge(parts_done, j + 1)
                    low(0)
                    bias(1)
                    for q in range(1, Q):
                        high(q)
                        low(q)
                else:
                    for q in range(Q):
                        high(q)
                    bias(0)
                    sp.wait_ge(parts_done, j + 1)
                    settled(sp)
                    bias(1)
                    for q in range(Q):
                        low(q)

            def store(j):
                sp.wait_ge(y01_read, j + 1)
                settled(sp)
                sp.wait_ge(y23_read, j + 1)
                settled(sp)
                sp.dma_start(y_cols[bass.ds(j, 1)].rearrange("b t p s -> p b t s"), yb[:, None, :, :]
                             ).then_inc(y_stored, 16)

            load_rows(0, xs, xs_loaded)
            load_rows(1, xs_second, second_loaded)
            stack_up(0, 0, first=True)
            sp.wait_ge(gram_mm, 1)
            load_rows(2, xs, xs_loaded)

            def element(b, side, stat, nxt, fin):
                if stat:
                    load_next_rows(b + 3)
                load_cols(b)
                if nxt:
                    stack_up(b + 1, side)
                if fin:
                    store(b - 2)

            element(0, 1, True, True, False)
            element(1, 0, True, True, False)
            with sp.Fori(2, B - 3) as b:
                element(b, (b + 1) % 2, True, True, True)
            element(B - 3, (B - 2) % 2, False, True, True)
            element(B - 2, (B - 1) % 2, False, True, True)
            element(B - 1, 0, False, False, True)
            store(B - 2)
            for h, done in enumerate((y01_read, y23_read)):
                sp.wait_ge(done, B)
                sp.dma_start(y_cols[B - 1, 2 * h:2 * h + 2].rearrange("t p s -> p t s"), yb_end[:, 2 * h:2 * h + 2, :]
                             ).then_inc(y_stored, 16)
            sp.wait_ge(y_stored, 16 * (B + 1))

        @block.tensor
        def _(pe):
            def sum_rows(j):
                src = rows_of(pe, j)
                after(pe, vare_done, j)
                for ch in range(SC):
                    for hf in range(2):
                        k = 2 * ch + hf
                        mm = nc.tensor.matmul(bx[C * k:C * k + C, 0:CH], ones_m,
                                              src[:, ch, 8 * hf:8 * hf + 8, :].rearrange("p m c -> p (m c)"),
                                              start=True, stop=True)
                mm.then_inc(part_mm, 1)

            def mean(j):
                pe.wait_ge(part_done, j + 1)
                for hf in range(2):
                    mm = nc.tensor.matmul(bx[:, 4 * hf:4 * hf + 4], k_sb[:, MEAN + P * hf:MEAN + P * hf + P],
                                          part[:, :], start=True, stop=True)
                mm.then_inc(mean_mm, 1)

            def gram_of(j):
                pe.wait_ge(mean_done, j + 1)
                pe.wait_ge(centred, j + 1)
                if isinstance(j, int) and j == 0:
                    pe.wait_ge(centred_by_dve, 1)
                    pe.wait_ge(set_zeros, 1)
                for t in range(T):
                    for ch in range(SC):
                        for q in range(Q):
                            mm = nc.tensor.matmul(bx[C * q:C * q + C, (C + 1) * t:(C + 1) * (t + 1)],
                                                  xc[:, ch, Q * t + q, 0:C], xc[:, ch, Q * t + q, :],
                                                  start=(ch == 0), stop=(ch == SC - 1))
                mm.then_inc(gram_mm, 1)

            def variance(j):
                pe.wait_ge(gram_done, j + 1)
                pe.wait_ge(trace_done, j + 1)
                nc.tensor.matmul(bx[:, 0:T], same_m, trace[:, :], start=True, stop=True).then_inc(var_mm, 1)

            def t_product(j, first, done, dst=bz):
                pe.wait_ge(gblk_done, j + 1)
                if first == 0:
                    settled(pe)
                elif dst is bz:
                    pe.wait_ge(t01_done, j + 1)
                for i in range(2):
                    mm = nc.tensor.matmul(dst[:, CH * i:CH * i + CH],
                                          gblk[:, first + i].rearrange("p q c -> p (q c)"), wk_sb[:, :],
                                          start=True, stop=True)
                mm.then_inc(done, 1)

            def tb_product(j):
                pe.wait_ge(sblk_done, j + 1)
                after(pe, beff_done, j - 2)
                settled(pe)
                nc.tensor.matmul(by[0:2 * M, 0:CH], sblk[:, :, :, :].rearrange("p k q t -> p (k q t)"), wk_sb[:, :],
                                 start=True, stop=True).then_inc(tb_mm, 1)

            def score(b, p, side):
                pe.wait_ge(stacked[p % Q], 32 * (b + 1))
                pe.wait_ge(bias_stacked, 32 * (b + 1))
                n = M * b + p
                after(pe, exped, n - NS + 1)
                settled(pe)
                for h in range(HC):
                    mm = nc.tensor.matmul(s_bank[p % NS][:, CH * h:CH * h + CH], wq_st[:, P * h:P * h + P],
                                          stack[:, side, p % Q, p // Q, :], start=True, stop=True)
                mm.then_inc(scores, 1)

            def column_sums(b, t):
                pe.wait_ge(inverted, T * b + t + 1)
                if t == 0:
                    after(pe, acc_read, b)
                for h in range(HC):
                    for q in range(Q):
                        mm = nc.tensor.matmul(acc[C * q:C * q + C, 0:CH], recip[:, t, q, h, :],
                                              e_sb[:, (Q * t + q) % NE, h, :],
                                              start=(t == 0 and h == 0), stop=(t == T - 1 and h == HC - 1))
                mm.then_inc(summed, 1)

            def a_columns(j):
                pe.wait_ge(acc_read, j + 1)
                pe.wait_ge(tb_done, min(j + 3, B) if isinstance(j, int) else j + 3)
                for h in range(HC):
                    mm = nc.tensor.matmul(by[:, M * h:M * h + M], a_sb[:, P * h:P * h + P], pick_m,
                                          start=True, stop=True)
                mm.then_inc(a_mm, 1)

            def weights(j):
                pe.wait_ge(ws_done, j + 1)
                for h in range(HC):
                    for q in range(Q):
                        nc.tensor.matmul(by[C * q:C * q + C, 0:T * C], wv_sb[:, h, :], ws[:, h, :, q, :],
                                         start=(h == 0), stop=(h == HC - 1))
                for h in range(HC):
                    mm = nc.tensor.matmul(by[:, P:P + M], wobv[:, h].rearrange("p q c -> p (q c)"), aT[:, h, :],
                                          start=(h == 0), stop=(h == HC - 1))
                mm.then_inc(w_mm, 1)

            def y_product(j, side, first, done, dst=bz):
                pe.wait_ge(wblk_done, j + 1)
                pe.wait_ge(xcT_done, j + 1)
                if first == 0:
                    pe.wait_ge(t23_done, min(j + 4, B) if isinstance(j, int) else j + 4)
                    if isinstance(j, int) and j > B - 4:
                        pe.wait_ge(y01_read, j)
                        pe.wait_ge(y23_read, j)
                elif dst is bz:
                    pe.wait_ge(y01_read, j + 1)
                else:
                    pe.wait_ge(y23_read, j)
                settled(pe)
                for i in range(2):
                    mm = nc.tensor.matmul(dst[:, S * i:S * i + S],
                                          wblk[:, first + i].rearrange("p q c -> p (q c)"),
                                          xcT[:, side, first + i, :], start=True, stop=True)
                mm.then_inc(done, 1)

            def element(b, side, sums, stat, nxt, out, fin, first=False, last=False):
                at = slots(first, last)
                for p in range(M):
                    if p + AHEAD < M:
                        score(b, p + AHEAD, side)
                    elif nxt:
                        score(b + 1, p + AHEAD - M, 1 - side)
                    if nxt and p == at["t01_product"]:
                        t_product(b + 1, 0, t01_mm)
                    if first and p == at["sum_rows_2"]:
                        sum_rows(b + 2)
                    if out and p == at["column_sums"]:
                        column_sums(b - 1, T - 1)
                    if nxt and p == at["t23_product"]:
                        t_product(b + 1, 2, t23_mm)
                    if first and p == at["mean_2"]:
                        mean(b + 2)
                    if nxt and p == at["tb_product"]:
                        tb_product(b + 1)
                    if out and p == at["a_columns"]:
                        a_columns(b - 1)
                    if stat and p == at["gram"]:
                        gram_of(b + 2)
                    if p % Q == at["column_sums"] and p >= Q:
                        column_sums(b, p // Q - 1)
                    if fin and p == at["y01_product"]:
                        y_product(b - 2, side, 0, y01_mm)
                    if stat and p == at["variance"]:
                        variance(b + 2)
                    if fin and p == at["y23_product"]:
                        y_product(b - 2, side, 2, y23_mm, dst=bx if last else bz)
                    if out and p == at["weights"]:
                        weights(b - 1)
                    if sums and p == at["sum_rows"]:
                        sum_rows(b + 3)
                    if sums and p == at["mean"]:
                        mean(b + 3)

            pe.wait_ge(k_loaded, 16)
            sum_rows(0)
            mean(0)
            gram_of(0)
            variance(0)
            sum_rows(1)
            pe.wait_ge(w_loaded, 16 * 7)
            t_product(0, 0, t01_mm)
            mean(1)
            tb_product(0)
            t_product(0, 2, t23_mm, dst=s_bank[0])
            gram_of(1)
            variance(1)
            pe.wait_ge(set_dve, 2)
            for p in range(AHEAD):
                score(0, p, 0)
            element(0, 0, True, True, True, False, False, first=True)
            element(1, 1, True, True, True, True, False)
            with pe.Fori(2, B - 3) as b:
                element(b, b % 2, True, True, True, True, True)
            element(B - 3, (B - 3) % 2, False, True, True, True, True)
            element(B - 2, (B - 2) % 2, False, False, True, True, True)
            element(B - 1, (B - 1) % 2, False, False, False, True, True, last=True)
            y_product(B - 2, (B - 2) % 2, 0, y01_mm)
            column_sums(B - 1, T - 1)
            a_columns(B - 1)
            y_product(B - 2, (B - 2) % 2, 2, y23_mm, dst=bx)
            weights(B - 1)
            y_product(B - 1, (B - 1) % 2, 0, y01_mm)
            y_product(B - 1, (B - 1) % 2, 2, y23_mm, dst=bx)

        @block.vector
        def _(dve):
            def sum_groups(j):
                dve.wait_ge(part_mm, j + 1)
                nc.vector.tensor_reduce(part[:, :], bx[:, 0:CH].rearrange("p (g e) -> p g e", g=G // 2),
                                        op=ALU.add, axis=AX.X).then_inc(part_done, 1)

            def read_mean(j):
                dve.wait_ge(mean_mm, j + 1)
                after(dve, centred, j)
                nc.vector.tensor_copy(nm[:, :], bx[:, 0:G])
                means = bx[:, 0:G].rearrange("p (t k) -> p t k", k=2)
                for k in range(2):
                    rows = slice(2 * C * k, 2 * C * (k + 1))
                    last = nc.vector.tensor_copy(nmT[rows, bass.ds(j, 1), :], means[rows, None, :, k])
                last.then_inc(mean_done, 1)

            def read_gram(j):
                dve.wait_ge(gram_mm, j + 1)
                after(dve, sblk_done, j)
                nc.vector.tensor_copy(gram[:, :, :].rearrange("p t c -> p (t c)"),
                                      bx[:, 0:T * (C + 1)]).then_inc(gram_done, 1)

            def sum_diagonal(j):
                dve.wait_ge(diag_done, j + 1)
                nc.vector.tensor_reduce(trace[:, :], gdiag[:, :, :], op=ALU.add, axis=AX.X).then_inc(trace_done, 1)

            def read_variance(j):
                dve.wait_ge(var_mm, j + 1)
                nc.vector.tensor_scalar(vare[:, :], bx[:, 0:T], EPS, None, ALU.add).then_inc(vare_done, 1)
                dve.wait_ge(vare_done, j + 1)
                nc.vector.reciprocal(rs2[:, :], vare[:, :]).then_inc(var_done, 1)

            def read_t(j, first, ready, done, src=bz):
                dve.wait_ge(ready, j + 1)
                dve.wait_ge(sblk_done, j + 1)
                after(dve, parts_done, j)
                for i in range(2):
                    last = nc.vector.scalar_tensor_tensor(t_sb[:, first + i, :], bk_sb[:, :],
                                                          ssum[:, first + i:first + i + 1],
                                                          src[:, CH * i:CH * i + CH], ALU.mult, ALU.add)
                last.then_inc(done, 1)

            def read_tb(j):
                dve.wait_ge(tb_mm, j + 1)
                after(dve, parts_done, j)
                nc.vector.scalar_tensor_tensor(t_sb[0:2 * M, T, :], bk_sb[0:2 * M, :], rows_all[0:2 * M, :],
                                               by[0:2 * M, 0:CH], ALU.mult, ALU.add).then_inc(tb_done, 1)

            def high_part(j):
                dve.wait_ge(t23_done, j + 1)
                dve.wait_ge(tb_done, j + 1)
                nc.vector.tensor_copy(t_parts[:, 0].rearrange("p t n -> p (t n)"),
                                      t_sb[:, :, :].rearrange("p t n -> p (t n)")).then_inc(hi_done, 1)

            def maximum(b, p):
                dve.wait_ge(scores, M * b + p + 1)
                nc.vector.tensor_reduce(negmax[:, p % NS, :],
                                        s_bank[p % NS][:, :].rearrange("p (h n) -> p h n", h=HC),
                                        op=ALU.max, axis=AX.X, negate=True).then_inc(maxed, 1)

            def invert(b, t):
                dve.wait_ge(exped, M * b + Q * (t + 1))
                nc.vector.reciprocal(recip[:, t, :, :, t], rowsum[:, t % 2, :, :]).then_inc(inverted, 1)

            def read_acc(j):
                dve.wait_ge(summed, T * (j + 1))
                after(dve, a_mm, j)
                nc.vector.tensor_copy(a_sb[:, :], acc[:, 0:CH]).then_inc(acc_read, 1)

            def read_a(j):
                dve.wait_ge(a_mm, j + 1)
                after(dve, w_mm, j)
                nc.vector.tensor_copy(aT[:, :, :].rearrange("p h m -> p (h m)"),
                                      by[:, 0:HC * M]).then_inc(a_done, 1)

            def read_weights(j, last_element=False):
                dve.wait_ge(w_mm, j + 1)
                dve.wait_ge(rs_done, j + 1)
                after(dve, wblk_done, j)
                after(dve, y01_read, j)
                after(dve, y23_read, j)
                nc.vector.tensor_tensor(wn[:, :, :], by[:, 0:T * C].rearrange("p (t c) -> p t c", t=T),
                                        rs[:, bass.ds(j, 1), :].rearrange("p b t -> p (b t)")[:, :, None]
                                        .to_broadcast([P, T, C]), ALU.mult).then_inc(wn_done, 1)
                if not last_element:
                    read_bias(j)
                dve.wait_ge(wn_done, j + 1)
                nc.vector.tensor_tensor(wf[:, :, :], wn[:, :, :], diag_m[:, None, :].to_broadcast([P, T, C]),
                                        ALU.add).then_inc(wf_done, 1)
                if last_element:
                    weight_blocks_last(j)
                    read_bias(j)

            def read_bias(j):
                for q in range(Q):
                    rows = slice(C * q, C * q + C)
                    bias = by[rows, P:P + M].rearrange("p (t q) -> p t q", q=Q)[:, :, q]
                    last = nc.vector.scalar_tensor_tensor(
                        beff[rows, :], bias, bo_sb[rows, :],
                        nmT[rows, bass.ds(j, 1), :].rearrange("p b t -> p (b t)"), ALU.add, ALU.subtract)
                last.then_inc(beff_done, 1)

            def read_y23(j, src=bz, dst=yb):
                dve.wait_ge(y23_mm, j + 1)
                dve.wait_ge(beff_done, j + 1)
                if dst is yb:
                    dve.wait_ge(y01_read, j + 1)
                nc.vector.tensor_tensor(dst[:, 2:4, :], src[:, :].rearrange("p (i s) -> p i s", i=2),
                                        beff[:, 2:4, None].to_broadcast([P, 2, S]), ALU.add).then_inc(y23_read, 1)

            def element(b, sums, stat, nxt, out, fin, first=False, last=False):
                at = slots(first, last)
                for p in range(M):
                    if p + LEAD < M:
                        maximum(b, p + LEAD)
                    elif nxt:
                        maximum(b + 1, p + LEAD - M)
                    if out and p == at["invert"]:
                        invert(b - 1, T - 1)
                    if p % Q == at["invert"] and p >= Q:
                        invert(b, p // Q - 1)
                    if stat and not first and p == at["read_mean"]:
                        read_mean(b + 2)
                    if nxt and p == at["read_t01"]:
                        read_t(b + 1, 0, t01_mm, t01_done)
                    if first and p == at["sum_groups_2"]:
                        sum_groups(b + 2)
                    if out and p == at["read_acc"]:
                        read_acc(b - 1)
                    if nxt and p == at["read_t23"]:
                        read_t(b + 1, 2, t23_mm, t23_done)
                    if first and p == at["read_mean_2"]:
                        read_mean(b + 2)
                    if nxt and p == at["read_tb"]:
                        read_tb(b + 1)
                    if nxt and p == at["high_part"]:
                        high_part(b + 1)
                    if out and p == at["read_a"]:
                        read_a(b - 1)
                    if stat and p == at["read_gram"]:
                        read_gram(b + 2)
                    if stat and p == at["sum_diagonal"]:
                        sum_diagonal(b + 2)
                    if stat and p == at["read_variance"]:
                        read_variance(b + 2)
                    if fin and p == at["read_y23"]:
                        read_y23(b - 2, src=bx if last else bz)
                    if out and p == at["read_weights"]:
                        read_weights(b - 1)
                    if sums and p == at["sum_groups"]:
                        sum_groups(b + 3)

            def centre_first():
                dve.wait_ge(mean_done, 1)
                shift = nm[:, :, None, None].to_broadcast([P, G, M // G, C])
                nc.vector.tensor_tensor(xc[:, 0, :, 0:C].rearrange("p (g k) c -> p g k c", g=G),
                                        xs[:, 0, :, :].rearrange("p (g k) c -> p g k c", g=G), shift, ALU.add
                                        ).then_inc(centred_by_dve, 1)

            def split_wq():
                dve.wait_ge(w_loaded, 16 * 7)
                nc.vector.tensor_copy(wq_hi[:, :], wq_raw[:, :]).then_inc(set_dve, 1)
                dve.wait_ge(set_dve, 1)
                nc.vector.scalar_tensor_tensor(wq_st[:, :], wq_hi[:, :].bitcast(f32),
                                               k_sb[0:ST, LOMASK:LOMASK + 1], wq_raw[:, :], ALU.mult, ALU.add
                                               ).then_inc(set_dve, 1)

            def diagonal_first():
                dve.wait_ge(gram_mm, 1)
                nc.vector.tensor_tensor(gdiag[:, :, :], bx[:, 0:T * (C + 1)].rearrange("p (t c) -> p t c", t=T)[:, :, 0:C],
                                        diag_m[:, None, :].to_broadcast([P, T, C]), ALU.mult
                                        ).then_inc(diag_done, 1)

            def blocks_first():
                dve.wait_ge(var_done, 1)
                nc.vector.tensor_tensor(gnorm[:, :, :], gram[:, :, 0:C], rs2[:, :, None].to_broadcast([P, T, C]),
                                        ALU.mult).then_inc(gnorm_done, 1)
                dve.wait_ge(gnorm_done, 1)
                nc.vector.tensor_tensor(gblk[:, :, :, :], gnorm[:, :, None, :].to_broadcast([P, T, Q, C]),
                                        own_m[:, None, :, None].to_broadcast([P, T, Q, C]), ALU.mult
                                        ).then_inc(gblk_done, 1)

            def low_part_first():
                dve.wait_ge(hi_done, 1)
                nc.vector.tensor_tensor(t_parts[:, 1], t_sb[:, :, :], t_parts[:, 0].bitcast(f32), ALU.subtract
                                        ).then_inc(parts_done, 1)

            dve.wait_ge(k_loaded, 16)
            sum_groups(0)
            read_mean(0)
            centre_first()
            split_wq()
            diagonal_first()
            read_gram(0)
            sum_diagonal(0)
            read_variance(0)
            blocks_first()
            sum_groups(1)
            read_t(0, 0, t01_mm, t01_done)
            read_mean(1)
            dve.wait_ge(set_pool, 1)
            read_tb(0)
            read_t(0, 2, t23_mm, t23_done, src=s_bank[0])
            high_part(0)
            low_part_first()
            read_gram(1)
            sum_diagonal(1)
            read_variance(1)
            for p in range(LEAD):
                maximum(0, p)
            element(0, True, True, True, False, False, first=True)
            element(1, True, True, True, True, False)
            with dve.Fori(2, B - 3) as b:
                element(b, True, True, True, True, True)
            element(B - 3, False, True, True, True, True)
            element(B - 2, False, False, True, True, True)
            element(B - 1, False, False, False, True, True, last=True)
            def scale_wo_last(j):
                dve.wait_ge(a_done, j + 1)
                dve.wait_ge(w_mm, j)
                nc.vector.tensor_tensor(ws[:, :, :, :, :].rearrange("p h t q c -> p h (t q) c"),
                                        wo_sb[:, :, None, :].to_broadcast([P, HC, M, C]),
                                        aT[:, :, :, None].to_broadcast([P, HC, M, C]), ALU.mult
                                        ).then_inc(ws_done, 1)

            def weight_blocks_last(j):
                dve.wait_ge(wf_done, j + 1)
                dve.wait_ge(y23_mm, j)
                nc.vector.tensor_tensor(wblk[:, :, :, :], wf[:, :, None, :].to_broadcast([P, T, Q, C]),
                                        own_m[:, None, :, None].to_broadcast([P, T, Q, C]), ALU.mult
                                        ).then_inc(wblk_done, 1)

            invert(B - 1, T - 1)
            read_acc(B - 1)
            read_a(B - 1)
            scale_wo_last(B - 1)
            read_y23(B - 2, src=bx)
            read_weights(B - 1, last_element=True)
            read_y23(B - 1, src=bx, dst=yb_end)

        @block.scalar
        def _(act):
            def exponentials(b, p):
                n = M * b + p
                act.wait_ge(maxed, n + 1)
                if p % Q == 0:
                    after(act, summed, T * b + p // Q - 1)
                for h in range(HC):
                    last = nc.scalar.activation(e_sb[:, p % NE, h, :], s_bank[p % NS][:, CH * h:CH * h + CH],
                                                ACT.Exp, bias=negmax[:, p % NS, h:h + 1],
                                                accum_out=rowsum[:, p // Q % 2, p % Q, h:h + 1])
                last.then_inc(exped, 1)

            def read_y01(j, dst=yb):
                act.wait_ge(y01_mm, j + 1)
                act.wait_ge(beff_done, j + 1)
                if dst is yb:
                    after(act, y_stored, 16 * j)
                for i in range(2):
                    last = nc.scalar.activation(dst[:, i, :], bz[:, S * i:S * i + S], ACT.Identity,
                                                bias=beff[:, i:i + 1])
                last.then_inc(y01_read, 1)

            def element(b, fin, first=False, last=False):
                at = slots(first, last)
                for p in range(M):
                    exponentials(b, p)
                    if fin and p == at["read_y01"]:
                        read_y01(b - 2)

            act.dma_start(k_sb[:, :], consts).then_inc(k_loaded, 16)
            for dst, src in ((wk_sb, wk_rep), (wq_raw, wq_stack), (bk_sb, bk_rep),
                             (bv_sb, bv), (bo_sb, bo_rep)):
                act.dma_start(dst[:, :], src).then_inc(w_loaded, 16)
            for dst, src in ((wo_sb, wo), (wv_sb, wv)):
                act.dma_start(dst[:, :, :], src.rearrange("(h p) c -> p h c", p=P)).then_inc(w_loaded, 16)
            nc.scalar.preload_act_table(ACT.Exp)
            element(0, False, first=True)
            element(1, False)
            element(2, True)
            with act.Fori(3, B - 2) as b:
                element(b, True)
            element(B - 2, True)
            element(B - 1, True, last=True)
            read_y01(B - 2)
            read_y01(B - 1, dst=yb_end)

        @block.gpsimd
        def _(pool):
            def centre_rows(j, chunks=range(SC)):
                pool.wait_ge(mean_done, j + 1)
                src = rows_of(pool, j)
                after(pool, gram_mm, j)
                for ch in chunks:
                    shift = nm[:, :, None, None].to_broadcast([P, G, M // G, C])
                    last = nc.gpsimd.tensor_tensor(
                        xc[:, ch, :, 0:C].rearrange("p (g k) c -> p g k c", g=G),
                        src[:, ch, :, :].rearrange("p (g k) c -> p g k c", g=G), shift, ALU.add)
                last.then_inc(centred, 1)

            def diagonal(j):
                pool.wait_ge(gram_done, j + 1)
                after(pool, trace_done, j)
                nc.gpsimd.tensor_tensor(gdiag[:, :, :], gram[:, :, 0:C],
                                        diag_m[:, None, :].to_broadcast([P, T, C]), ALU.mult
                                        ).then_inc(diag_done, 1)

            def gram_blocks(j):
                pool.wait_ge(var_done, j + 1)
                nc.gpsimd.tensor_tensor(gnorm[:, :, :], gram[:, :, 0:C],
                                        rs2[:, :, None].to_broadcast([P, T, C]), ALU.mult).then_inc(gnorm_done, 1)
                pool.wait_ge(gnorm_done, j + 1)
                after(pool, t23_mm, j)
                settled(pool)
                nc.gpsimd.tensor_tensor(gblk[:, :, :, :], gnorm[:, :, None, :].to_broadcast([P, T, Q, C]),
                                        own_m[:, None, :, None].to_broadcast([P, T, Q, C]), ALU.mult
                                        ).then_inc(gblk_done, 1)

            def sum_blocks(j):
                pool.wait_ge(var_done, j + 1)
                nc.gpsimd.tensor_tensor(rs_now[:, :], vare[:, :], half[:, :], ALU.pow).then_inc(std_done, 1)
                pool.wait_ge(std_done, j + 1)
                after(pool, tb_mm, j)
                after(pool, t23_done, j)
                settled(pool)
                nc.gpsimd.tensor_tensor(ssum[:, :], gram[:, :, C], rs_now[:, :], ALU.mult).then_inc(ssum_done, 1)
                nc.gpsimd.tensor_copy(rs[:, bass.ds(j, 1), :], rs_now[:, None, :]).then_inc(rs_done, 1)
                pool.wait_ge(ssum_done, j + 1)
                nc.gpsimd.tensor_tensor(sblk[:, :, :, :], ssum[:, None, None, :].to_broadcast([P, 2, Q, T]),
                                        own_m[:, None, :, None].to_broadcast([P, 2, Q, T]), ALU.mult
                                        ).then_inc(sblk_done, 1)

            def low_part(j):
                pool.wait_ge(hi_done, j + 1)
                nc.gpsimd.tensor_tensor(t_parts[:, 1], t_sb[:, :, :], t_parts[:, 0].bitcast(f32), ALU.subtract
                                        ).then_inc(parts_done, 1)

            def centre_cols(j, side):
                pool.wait_ge(xT_loaded, 16 * (j + 1))
                pool.wait_ge(mean_done, j + 1)
                settled(pool)
                shift = nmT[:, bass.ds(j, 1), :].rearrange("p b t -> p (b t)")[:, :, None].to_broadcast([P, T, S])
                nc.gpsimd.tensor_tensor(xcT[:, side, :, :], xT[:, :, :], shift, ALU.add).then_inc(xcT_done, 1)

            def scale_wo(j):
                pool.wait_ge(a_done, j + 1)
                after(pool, w_mm, j)
                nc.gpsimd.tensor_tensor(ws[:, :, :, :, :].rearrange("p h t q c -> p h (t q) c"),
                                        wo_sb[:, :, None, :].to_broadcast([P, HC, M, C]),
                                        aT[:, :, :, None].to_broadcast([P, HC, M, C]), ALU.mult
                                        ).then_inc(ws_done, 1)

            def weight_blocks(j):
                pool.wait_ge(wf_done, j + 1)
                settled(pool)
                nc.gpsimd.tensor_tensor(wblk[:, :, :, :], wf[:, :, None, :].to_broadcast([P, T, Q, C]),
                                        own_m[:, None, :, None].to_broadcast([P, T, Q, C]), ALU.mult
                                        ).then_inc(wblk_done, 1)

            nc.gpsimd.memset(half[:, :], -0.5)
            nc.gpsimd.memset(rows_all[:, :], float(S))
            nc.gpsimd.memset(t_sb[:, T, :], 0.0)
            nc.gpsimd.memset(xc[:, :, :, C:C + 1], 1.0).then_inc(set_zeros, 1)
            nc.gpsimd.memset(recip[:, :, :, :, :], 0.0).then_inc(set_zeros, 1)
            centre_rows(0, chunks=(1,))
            pool.wait_ge(w_loaded, 16 * 7)
            for h in range(HC):
                last = nc.gpsimd.tensor_scalar(wobv[:, h], wo_sb[:, h, None, :].to_broadcast([P, Q, C]),
                                               bv_sb[:, h:h + 1], 0.0, ALU.mult, ALU.add)
            last.then_inc(set_pool, 1)
            sum_blocks(0)
            centre_rows(1)
            diagonal(1)

            def element(b, side, stat, nxt, out, fin, first=False):
                if first:
                    gram_blocks(1)
                    sum_blocks(1)
                if fin:
                    weight_blocks(b - 2)
                if out:
                    centre_cols(b - 1, 1 - side)
                if stat:
                    centre_rows(b + 2)
                    diagonal(b + 2)
                if nxt:
                    low_part(b + 1)
                if out:
                    scale_wo(b - 1)
                if stat:
                    gram_blocks(b + 2)
                    sum_blocks(b + 2)

            element(0, 0, True, True, False, False, first=True)
            element(1, 1, True, True, True, False)
            with pool.Fori(2, B - 2) as b:
                element(b, b % 2, True, True, True, True)
            element(B - 2, (B - 2) % 2, False, True, True, True)
            element(B - 1, (B - 1) % 2, False, False, True, True)
            weight_blocks(B - 2)
            centre_cols(B - 1, (B - 1) % 2)


def kernel(x, L0_conv_Wq, L0_conv_bq, L0_conv_Wk, L0_conv_bk, L0_conv_Wv, L0_conv_bv, L0_conv_Wo, L0_conv_bo):
    import concourse.bacc as bacc
    from concourse.bass_utils import run_bass_kernel_spmd

    x, wq, bq, wk, bk, wv, bv, wo, bo = (np.asarray(a) for a in (
        x, L0_conv_Wq, L0_conv_bq, L0_conv_Wk, L0_conv_bk, L0_conv_Wv, L0_conv_bv, L0_conv_Wo, L0_conv_bo))
    arrays = {
        "x_rows": x.transpose(0, 1, 3, 2),
        "x_cols": x.transpose(0, 3, 2, 1).reshape(B, T, P, S),
        "wq_stack": np.concatenate([np.repeat(wq.T, 2, axis=0), wq.T, np.repeat(bq[None], NP, axis=0)]),
        "wk_rep": np.concatenate([wk.T] * Q),
        "bk_rep": np.broadcast_to(bk, (P, CH)),
        "wv": wv,
        "wo": wo.T,
        "bv": bv.reshape(HC, P).T,
        "bo_rep": np.tile(bo, Q)[:, None],
        "consts": shape_constants(),
    }
    arrays = {name: np.ascontiguousarray(a) for name, a in arrays.items()}
    nc = bacc.Bacc("TRN2", target_bir_lowering=False, num_devices=1)
    args = [nc.dram_tensor(name, a.shape, mybir.dt.from_np(a.dtype), kind="ExternalInput").ap()
            for name, a in arrays.items()]
    y = nc.dram_tensor("y_cols", (B, T, P, S), mybir.dt.float32, kind="ExternalOutput").ap()
    build(nc, *args, y)
    r = run_bass_kernel_spmd(nc, [arrays], core_ids=[0])
    return r.results[0]["y_cols"].reshape(B, M, C, S).transpose(0, 3, 2, 1)
```
